# Optimizing a Trainium2 kernel written in Bass

```python
import numpy as np
import jax
import jax.numpy as jnp

def _softmax(x, axis=-1):
    return jax.nn.softmax(x, axis=axis)

def _gelu(x):
    return jax.nn.gelu(x, approximate=True)

def _silu(x):
    return jax.nn.silu(x)

def _sigmoid(x):
    return jax.nn.sigmoid(x)

def _layernorm(x, axis=-1, eps=1e-05):
    m = jnp.mean(x, axis=axis, keepdims=True)
    v = jnp.var(x, axis=axis, keepdims=True)
    return (x - m) / jnp.sqrt(v + eps)

def _scatter_add(tgt, idx, src, axis=0):
    return tgt.at[idx].add(src)

def _segment_sum(src, seg, n):
    return jax.ops.segment_sum(src, seg, n)
kernel_name = 'mk_gnn_preln_d1_gnn_r64_9ec9bb'

def setup_inputs(seed: int=0):
    np.random.seed(seed)
    _w = jnp.asarray

    def _rec_inputs():
        import jax
        import jax.numpy as jnp
        _gk = jax.random.key(seed)
        x = -8.776e-05 + 1 * jax.random.normal(jax.random.fold_in(_gk, 1), (10000, 512), jnp.float32)
        src = jax.random.randint(jax.random.fold_in(_gk, 2), (5000,), 0, 10000, jnp.int32)
        dst = jax.random.randint(jax.random.fold_in(_gk, 3), (5000,), 0, 10000, jnp.int32)
        _o = jnp.argsort(dst, stable=True)
        src = src[_o]
        dst = dst[_o]
        return (x, src, dst)
    x, src, dst = _rec_inputs()

    def _L0_gnn_setup():
        import jax, jax.numpy as jnp
        import numpy as np
        N = 10000
        E = 2500
        D = 512
        EPS = 1e-05

        def _lin_params(key, out_d, in_d, bias=True):
            k1, k2 = jax.random.split(key)
            s = 1.0 / np.sqrt(in_d)
            W = jax.random.uniform(k1, (out_d, in_d), jnp.float32, -s, s)
            if bias:
                b = jax.random.uniform(k2, (out_d,), jnp.float32, -s, s)
                return (W, b)
            return (W,)

        def _sage_conv(x, src, dst, Wp, bp, Wl, bl, Wr):
            h = jax.nn.relu(x @ Wp.T + bp)
            agg = jax.ops.segment_sum(h[src], dst, num_segments=N)
            cnt = jax.ops.segment_sum(jnp.ones((src.shape[0],), x.dtype), dst, num_segments=N)
            agg = agg / jnp.maximum(cnt, 1.0)[:, None]
            return agg @ Wl.T + bl + x @ Wr.T

        def _relu_ln(x, g, b):
            x = jax.nn.relu(x)
            mu = jnp.mean(x, axis=-1, keepdims=True)
            var = jnp.mean(jnp.square(x - mu), axis=-1, keepdims=True)
            return (x - mu) * jax.lax.rsqrt(var + EPS) * g + b
        key = jax.random.key(seed)
        ks = jax.random.split(key, 16)
        inp = {'x': jax.random.normal(ks[0], (N, D), jnp.float32), 'edge_index': jax.random.randint(ks[1], (2, E), 0, N, jnp.int64)}
        ki = 2
        for l in range(3):
            Wp, bp = _lin_params(ks[ki], D, D)
            ki += 1
            Wl, bl = _lin_params(ks[ki], D, D)
            ki += 1
            Wr, = _lin_params(ks[ki], D, D, bias=False)
            ki += 1
            inp[f'Wp{l}'] = Wp
            inp[f'bp{l}'] = bp
            inp[f'Wl{l}'] = Wl
            inp[f'bl{l}'] = bl
            inp[f'Wr{l}'] = Wr
            if l < 2:
                inp[f'g{l}'] = jnp.ones((D,), jnp.float32)
                inp[f'be{l}'] = jnp.zeros((D,), jnp.float32)
        return inp
    _L0_gnn_all = _L0_gnn_setup()
    _L0_gnn_in = {k: v for k, v in _L0_gnn_all.items() if k in ('Wp0', 'bp0', 'Wl0', 'bl0', 'Wr0', 'g0', 'be0', 'Wp1', 'bp1', 'Wl1', 'bl1', 'Wr1', 'g1', 'be1', 'Wp2', 'bp2', 'Wl2', 'bl2', 'Wr2')}
    del _L0_gnn_all
    return {'x': x, 'src': src, 'dst': dst, 'L0_gnn_Wp0': _L0_gnn_in['Wp0'], 'L0_gnn_bp0': _L0_gnn_in['bp0'], 'L0_gnn_Wl0': _L0_gnn_in['Wl0'], 'L0_gnn_bl0': _L0_gnn_in['bl0'], 'L0_gnn_Wr0': _L0_gnn_in['Wr0'], 'L0_gnn_g0': _L0_gnn_in['g0'], 'L0_gnn_be0': _L0_gnn_in['be0'], 'L0_gnn_Wp1': _L0_gnn_in['Wp1'], 'L0_gnn_bp1': _L0_gnn_in['bp1'], 'L0_gnn_Wl1': _L0_gnn_in['Wl1'], 'L0_gnn_bl1': _L0_gnn_in['bl1'], 'L0_gnn_Wr1': _L0_gnn_in['Wr1'], 'L0_gnn_g1': _L0_gnn_in['g1'], 'L0_gnn_be1': _L0_gnn_in['be1'], 'L0_gnn_Wp2': _L0_gnn_in['Wp2'], 'L0_gnn_bp2': _L0_gnn_in['bp2'], 'L0_gnn_Wl2': _L0_gnn_in['Wl2'], 'L0_gnn_bl2': _L0_gnn_in['bl2'], 'L0_gnn_Wr2': _L0_gnn_in['Wr2']}

def reference(x, src, dst, L0_gnn_Wp0, L0_gnn_bp0, L0_gnn_Wl0, L0_gnn_bl0, L0_gnn_Wr0, L0_gnn_g0, L0_gnn_be0, L0_gnn_Wp1, L0_gnn_bp1, L0_gnn_Wl1, L0_gnn_bl1, L0_gnn_Wr1, L0_gnn_g1, L0_gnn_be1, L0_gnn_Wp2, L0_gnn_bp2, L0_gnn_Wl2, L0_gnn_bl2, L0_gnn_Wr2):
    import jax
    import jax.numpy as jnp

    def _L0_gnn_ref(x, edge_index, Wp0, bp0, Wl0, bl0, Wr0, g0, be0, Wp1, bp1, Wl1, bl1, Wr1, g1, be1, Wp2, bp2, Wl2, bl2, Wr2):
        import jax, jax.numpy as jnp
        import numpy as np
        N = 10000
        E = 2500
        D = 512
        EPS = 1e-05

        def _lin_params(key, out_d, in_d, bias=True):
            k1, k2 = jax.random.split(key)
            s = 1.0 / np.sqrt(in_d)
            W = jax.random.uniform(k1, (out_d, in_d), jnp.float32, -s, s)
            if bias:
                b = jax.random.uniform(k2, (out_d,), jnp.float32, -s, s)
                return (W, b)
            return (W,)

        def _sage_conv(x, src, dst, Wp, bp, Wl, bl, Wr):
            h = jax.nn.relu(x @ Wp.T + bp)
            agg = jax.ops.segment_sum(h[src], dst, num_segments=N)
            cnt = jax.ops.segment_sum(jnp.ones((src.shape[0],), x.dtype), dst, num_segments=N)
            agg = agg / jnp.maximum(cnt, 1.0)[:, None]
            return agg @ Wl.T + bl + x @ Wr.T

        def _relu_ln(x, g, b):
            x = jax.nn.relu(x)
            mu = jnp.mean(x, axis=-1, keepdims=True)
            var = jnp.mean(jnp.square(x - mu), axis=-1, keepdims=True)
            return (x - mu) * jax.lax.rsqrt(var + EPS) * g + b
        src, dst = (edge_index[0], edge_index[1])
        x = _sage_conv(x, src, dst, Wp0, bp0, Wl0, bl0, Wr0)
        x = _relu_ln(x, g0, be0)
        x = _sage_conv(x, src, dst, Wp1, bp1, Wl1, bl1, Wr1)
        x = _relu_ln(x, g1, be1)
        x = _sage_conv(x, src, dst, Wp2, bp2, Wl2, bl2, Wr2)
        return x
    edge_index = jnp.stack([src, dst])
    h = jnp.maximum(_layernorm(x, axis=-1), 0.0)
    x = x + _L0_gnn_ref(h, edge_index, L0_gnn_Wp0, L0_gnn_bp0, L0_gnn_Wl0, L0_gnn_bl0, L0_gnn_Wr0, L0_gnn_g0, L0_gnn_be0, L0_gnn_Wp1, L0_gnn_bp1, L0_gnn_Wl1, L0_gnn_bl1, L0_gnn_Wr1, L0_gnn_g1, L0_gnn_be1, L0_gnn_Wp2, L0_gnn_bp2, L0_gnn_Wl2, L0_gnn_bl2, L0_gnn_Wr2)
    return x

_drawn_inputs = setup_inputs


def setup_inputs(seed=0):
    import zlib

    import numpy as np

    out = dict(_drawn_inputs(seed))
    spreads = {'L0_gnn_g0': (1.0, 0.2),
     'L0_gnn_be0': (0.0, 0.1),
     'L0_gnn_g1': (1.0, 0.2),
     'L0_gnn_be1': (0.0, 0.1)}
    factors = {'L0_gnn_bp0': 5.17, 'L0_gnn_bp1': 8.0, 'L0_gnn_bp2': 8.0, 'L0_gnn_bl2': 2.723}
    for name, (base, spread) in spreads.items():
        noise = np.random.default_rng([zlib.crc32(name.encode()), seed]).standard_normal(out[name].shape)
        drawn = base * np.exp(spread * noise) if base else spread * noise
        out[name] = jnp.asarray(drawn.astype(out[name].dtype))
    for name, factor in factors.items():
        out[name] = (out[name] * factor).astype(out[name].dtype)
    return out
```

```python
from contextlib import ExitStack

import concourse.bass as bass
from concourse import mybir

P = 128
ALU = mybir.AluOpType
ACT = mybir.ActivationFunctionType
F32 = mybir.dt.float32
F32R = mybir.dt.float32r
BF16 = mybir.dt.bfloat16
I32 = mybir.dt.int32
EPS = 1e-5
LAYERS = 3
DMA = 16
EDGE_RING = 2
NODE_RING = 3


def sweep(eng, count, ring, low, high, body):
    first, end = 1 - low // ring, (count - high) // ring

    def written_out(i):
        body(i // ring, i % ring, lambda d: 0 <= i + d < count)

    for i in range(-high, first * ring):
        written_out(i)
    with eng.Fori(first, end) as j:
        for s in range(ring):
            body(j, s, lambda d: True)
    for i in range(end * ring, count - low):
        written_out(i)


def sage_kernel(nc, x_in, src_in, dst_in, weights, out):
    N, D = x_in.shape
    E = src_in.shape[0]
    K = D // P
    NODE_TILES = -(-N // P)
    LAST_ROWS = N - (NODE_TILES - 1) * P
    EDGE_TILES = -(-E // P)
    EDGES = EDGE_TILES * P
    EDGE_ROWS = E // EDGE_TILES
    PAD_NODE = NODE_TILES * P
    BIAS_ROW = EDGES
    assert D == 512 and EDGE_ROWS * EDGE_TILES == E and EDGE_ROWS <= P and NODE_TILES < P

    with ExitStack() as ctx:
        def sb(name, shape, dt):
            return ctx.enter_context(nc.sbuf_tensor(name, shape, dt))

        def sem(name):
            return ctx.enter_context(nc.semaphore(name))

        def sems(name, n):
            return [sem(f"{name}{i}") for i in range(n)]

        node_x = nc.dram_tensor("node_x", [NODE_TILES * P, D], F32).ap()
        edge_table = nc.dram_tensor("edge_table", [EDGES + 1, D], F32).ap()
        edge_records = nc.dram_tensor("edge_records", [EDGES, 4], F32).ap()

        bank = [ctx.enter_context(nc.psum_tensor(f"bank{i}", [P, 512], F32)) for i in range(8)]

        stage = {m: sb(f"stage_{m}", [P, K, D], F32) for m in "plr"}
        w_high = {m: sb(f"w_high_{m}", [P, K, D], F32R) for m in "plr"}
        w_low = {m: sb(f"w_low_{m}", [P, K, D], F32R) for m in "plr"}
        bias_stage = {m: sb(f"bias_stage_{m}", [P, D], F32) for m in "pl"}
        bias = {m: sb(f"bias_{m}", [P, D], F32) for m in "pl"}
        gain = sb("gain", [P, K], F32)
        shift = sb("shift", [P, K], F32)
        shift_cols = sb("shift_cols", [P, K, P], F32)

        ones = sb("ones", [P, P], F32)
        ident = sb("ident", [P, P], F32)
        below = sb("below", [P, P], F32)
        above = sb("above", [P, P], F32)
        upto = sb("upto", [P, P], F32)
        column_no = sb("column_no", [P, P], F32)
        partition_no = sb("partition_no", [P, 1], F32)
        eps = sb("eps", [P, 1], F32)

        dst_i = sb("dst_i", [P, EDGE_TILES], I32)
        src_i = sb("src_i", [P, EDGE_TILES], I32)
        hi_i = sb("hi_i", [P, EDGE_TILES], I32)
        lo_i = sb("lo_i", [P, EDGE_TILES], I32)
        dst_f = sb("dst_f", [P, EDGE_TILES], F32)
        hi_f = sb("hi_f", [P, EDGE_TILES], F32)
        lo_f = sb("lo_f", [P, EDGE_TILES], F32)
        hot_hi = sb("hot_hi", [P, EDGE_RING, P], F32)
        hot_lo = sb("hot_lo", [P, EDGE_RING, P], F32)
        hot_hi_b = sb("hot_hi_b", [P, EDGE_RING, P], BF16)
        hot_lo_b = sb("hot_lo_b", [P, EDGE_RING, P], BF16)
        diag = sb("diag", [P, EDGE_RING, 2, P], F32)
        hot_t = sb("hot_t", [P, EDGE_RING, P], F32)
        count_lh = sb("count_lh", [P, P], F32)
        table = sb("table", [P, 2, P], F32)
        start = sb("start", [P, P], F32)
        column_total = sb("column_total", [P, 1], F32)
        tile_start = sb("tile_start", [P, 1], F32)
        total_cols = sb("total_cols", [P, P], F32)
        scratch = sb("scratch", [P, P], F32)
        scratch2 = sb("scratch2", [P, P], F32)
        rank_start = sb("rank_start", [P, EDGE_TILES], F32)
        rank_in_tile = sb("rank_in_tile", [P, EDGE_TILES], F32)
        rank_f = sb("rank_f", [P, EDGE_TILES], F32)
        rank_i = sb("rank_i", [P, EDGE_TILES], I32)
        edge_count = sb("edge_count", [P, EDGE_TILES], F32)
        record = sb("record", [P, EDGE_TILES, 4], F32)
        scatter_rank = sb("scatter_rank", [P, EDGE_RING], I32)
        scatter_record = sb("scatter_record", [P, EDGE_RING, 4], F32)
        sorted_record = sb("sorted_record", [P, EDGE_TILES, 4], F32)
        sorted_src = sb("sorted_src", [P, EDGE_TILES], I32)
        dst_row = sb("dst_row", [P, 1 + EDGES], F32)
        has_edges = sb("has_edges", [P, P], F32)
        owner_f = sb("owner_f", [P, P], F32)
        owner_f2 = sb("owner_f2", [P, P], F32)
        owner = sb("owner", [P, P], I32)

        gathered = sb("gathered", [P, EDGE_RING, D], F32)
        gather_idx = sb("gather_idx", [P, EDGE_RING], I32)
        same = sb("same", [P, EDGE_RING, P], F32R)
        carries = sb("carries", [P, EDGE_RING, P], F32)
        h_pre = sb("h_pre", [P, D], F32)
        h_high = sb("h_high", [P, D], F32R)
        h_low = sb("h_low", [P, D], F32R)
        agg = sb("agg", [P, EDGE_RING, K, P], F32)
        agg_high = sb("agg_high", [P, K, P], F32R)
        agg_low = sb("agg_low", [P, K, P], F32R)
        edge_out = sb("edge_out", [P, EDGE_RING, D], F32)

        xt_high = sb("xt_high", [P, NODE_RING, K, P], F32R)
        xt_low = sb("xt_low", [P, NODE_RING, K, P], F32R)

        x_tile = sb("x_tile", [P, NODE_RING, D], F32)
        residual = sb("residual", [P, NODE_RING, D], F32)
        owner_idx = sb("owner_idx", [P, NODE_RING], I32)
        edge_row = sb("edge_row", [P, NODE_RING, D], F32)
        y = sb("y", [P, NODE_RING, D], F32)

        in_stats = sb("in_stats", [P, NODE_RING, 6], F32)
        in_mean = sb("in_mean", [P, NODE_RING, 2], F32)
        in_std = sb("in_std", [P, NODE_RING], F32)
        in_rstd = sb("in_rstd", [P, NODE_RING], F32)
        in_off = sb("in_off", [P, NODE_RING], F32)
        ln_stats = sb("ln_stats", [P, NODE_RING, 6], F32)
        ln_mean = sb("ln_mean", [P, NODE_RING, 2], F32)
        ln_std = sb("ln_std", [P, NODE_RING], F32)
        ln_rstd = sb("ln_rstd", [P, NODE_RING], F32)

        w_loaded = {m: sem(f"w_loaded_{m}") for m in "plr"}
        bias_loaded = {m: sem(f"bias_loaded_{m}") for m in "pl"}
        affine_loaded = sem("affine_loaded")
        w_high_done = {m: sem(f"w_high_done_{m}") for m in "plr"}
        w_low_done = {m: sem(f"w_low_done_{m}") for m in "plr"}
        shift_done = sem("shift_done")
        bias_product = {m: sem(f"bias_product_{m}") for m in "pl"}
        bias_done = {m: sem(f"bias_done_{m}") for m in "pl"}
        bias_stored = sem("bias_stored")

        consts = sem("consts")
        memset_done = sem("memset_done")
        pads_done = sem("pads_done")
        graph_loaded = sem("graph_loaded")
        digits = sem("digits")
        hot_done = sem("hot_done")
        counted = sem("counted")
        prep = sem("prep")
        prep_pe = sem("prep_pe")
        diag_done = sem("diag_done")
        row_done = sem("row_done")
        hot_t_done = sem("hot_t_done")
        hot2_done = sem("hot2_done")
        in_tile_done = sem("in_tile_done")
        table_copied = sem("table_copied")
        table_added = sem("table_added")
        looked_up = sem("looked_up")
        rank_read = sem("rank_read")
        records_ready = sem("records_ready")
        scatter_copied = sem("scatter_copied")
        scattered = sems("scattered", EDGE_RING)
        sorted_loaded = sem("sorted_loaded")
        sorted_ready = sem("sorted_ready")
        sdiag_done = sem("sdiag_done")
        srow_done = sem("srow_done")
        srow_copied = sem("srow_copied")
        owner_ready = sem("owner_ready")

        e_idx = sem("e_idx")
        e_gathered = sems("e_gathered", EDGE_RING)
        e_turned = sem("e_turned")
        e_xt_high = sem("e_xt_high")
        e_xt_low = sem("e_xt_low")
        e_projected = sem("e_projected")
        e_h_pre = sem("e_h_pre")
        e_h_high = sem("e_h_high")
        e_h_low = sem("e_h_low")
        e_masks = sem("e_masks")
        e_summed = sem("e_summed")
        e_agg = sem("e_agg")
        e_agg_high = sem("e_agg_high")
        e_agg_low = sem("e_agg_low")
        e_product = sem("e_product")
        e_out = sem("e_out")
        e_stored = sems("e_stored", EDGE_RING)

        n_loaded = sems("n_loaded", NODE_RING)
        n_residual = sems("n_residual", NODE_RING)
        n_idx = sem("n_idx")
        n_gathered = sems("n_gathered", NODE_RING)
        n_turned = sem("n_turned")
        n_xt_high = sem("n_xt_high")
        n_xt_low = sem("n_xt_low")
        n_product = sem("n_product")
        n_summed = sem("n_summed")
        n_relu = sem("n_relu")
        n_stats = sem("n_stats")
        n_mean = sem("n_mean")
        n_std = sem("n_std")
        n_rstd = sem("n_rstd")
        n_out = sem("n_out")
        n_stored = sems("n_stored", NODE_RING)

        in_s_stats = sem("in_s_stats")
        in_s_mean = sem("in_s_mean")
        in_s_std = sem("in_s_std")
        in_s_rstd = sem("in_s_rstd")
        in_s_off = sem("in_s_off")
        in_s_done = sem("in_s_done")

        def reach(eng, s, value):
            if not isinstance(value, int) or value > 0:
                eng.wait_ge(s, value)

        class Phase:

            def __init__(self, l, count, ring):
                self.l, self.count, self.ring = l, count, ring

            def at(self, j, s, d):
                return j * self.ring + (s + d), (s + d) % self.ring, j + (s + d) // self.ring

            def tiles(self, t):
                return t + (self.l * self.count + 1)

            def slot(self, slot, turn):
                per_layer = -(-(self.count - slot) // self.ring)
                return turn * DMA + (self.l * per_layer + 1) * DMA

        def edges(l):
            return Phase(l, EDGE_TILES, EDGE_RING)

        def nodes(l):
            return Phase(l, NODE_TILES, NODE_RING)

        def all_edge_rows_stored(eng, l):
            for s in range(EDGE_RING):
                eng.wait_ge(e_stored[s], DMA * (l + 1) * (-(-(EDGE_TILES - s) // EDGE_RING)))

        def all_nodes_stored(eng, l):
            for s in range(NODE_RING):
                eng.wait_ge(n_stored[s], DMA * (l + 1) * (-(-(NODE_TILES - s) // NODE_RING)))

        block = ctx.enter_context(nc.Block())

        @block.sync
        def _(sp):
            def load_weights(l, ms):
                for m in ms:
                    if l:
                        sp.wait_ge(w_low_done[m], l)
                        sp.wait_ge(w_high_done[m], l)
                        if l > 1 and m == "p":
                            sp.wait_ge(bias_product["p"], l - 1)
                        if l > 1 and m == "r":
                            sp.wait_ge(bias_product["l"], l - 1)
                    sp.dma_start(stage[m][:], weights[l]["W" + m].rearrange("(k p) n -> p k n", p=P)
                                 ).then_inc(w_loaded[m], DMA)

            def load_biases(l):
                for m in "pl":
                    if l:
                        sp.wait_ge(bias_done[m], l)
                    sp.dma_start(bias_stage[m][:], weights[l]["b" + m].rearrange("(a n) -> a n", a=1)
                                 .to_broadcast([P, D])).then_inc(bias_loaded[m], DMA)

            def load_affine(l):
                if l > 1:
                    sp.wait_ge(w_low_done["r"], l)
                    sp.wait_ge(w_high_done["r"], l)
                    sp.wait_ge(w_low_done["p"], l)
                    sp.wait_ge(shift_done, l - 1)
                for buf, name in ((gain, "g"), (shift, "be")):
                    sp.dma_start(buf[:], weights[l][name]).then_inc(affine_loaded, DMA)

            sp.wait_ge(pads_done, 2)
            sp.dma_start(dst_i[0:EDGE_ROWS, :], dst_in.rearrange("(p t) -> p t", t=EDGE_TILES)
                         ).then_inc(graph_loaded, DMA)
            sp.dma_start(src_i[0:EDGE_ROWS, :], src_in.rearrange("(p t) -> p t", t=EDGE_TILES)
                         ).then_inc(graph_loaded, DMA)
            load_weights(0, "plr")
            load_biases(0)
            for s in range(EDGE_RING):
                sp.wait_ge(scattered[s], DMA * EDGE_TILES // EDGE_RING)
            sp.dma_start(sorted_record[:], edge_records.rearrange("(t p) c -> p t c", p=P)
                         ).then_inc(sorted_loaded, DMA)

            for l in range(LAYERS):
                if l + 1 < LAYERS:
                    load_affine(l + 1)
                    load_weights(l + 1, "pl")
                sp.wait_ge(bias_done["l"], l + 1)
                sp.dma_start(edge_table[BIAS_ROW:BIAS_ROW + 1, :], bias["l"][0:1, :]
                             ).then_inc(bias_stored, DMA)
                ph = edges(l)

                def store_edges(j, s, alive):
                    t, slot, turn = ph.at(j, s, 0)
                    sp.wait_ge(e_out, ph.tiles(t))
                    sp.dma_start(edge_table[bass.ds(t * P, P), :], edge_out[:, slot, :]
                                 ).then_inc(e_stored[slot], DMA)

                sweep(sp, EDGE_TILES, EDGE_RING, 0, 0, store_edges)

                if l + 1 < LAYERS:
                    load_biases(l + 1)
                    load_weights(l + 1, "r")
                ph = nodes(l)
                source = x_in if l == 0 else node_x
                target = out if l == LAYERS - 1 else node_x

                def move_nodes(j, s, alive):
                    if alive(2):
                        t, slot, turn = ph.at(j, s, 2)
                        rows = P if not isinstance(t, int) or t < NODE_TILES - 1 or l else LAST_ROWS
                        reach(sp, n_turned, ph.tiles(t - NODE_RING))
                        sp.dma_start(x_tile[0:rows, slot, :], source[bass.ds(t * P, rows), :]
                                     ).then_inc(n_loaded[slot], DMA)
                        if l == LAYERS - 1:
                            rows = P if not isinstance(t, int) or t < NODE_TILES - 1 else LAST_ROWS
                            if not isinstance(t, int) or t >= NODE_RING:
                                sp.wait_ge(n_out, ph.tiles(t - NODE_RING))
                            sp.dma_start(residual[0:rows, slot, :], x_in[bass.ds(t * P, rows), :]
                                         ).then_inc(n_residual[slot], DMA)
                    if alive(-2):
                        t, slot, turn = ph.at(j, s, -2)
                        last = isinstance(t, int) and t == NODE_TILES - 1 and l == LAYERS - 1
                        rows = LAST_ROWS if last else P
                        sp.wait_ge(n_out, ph.tiles(t))
                        sp.dma_start(target[bass.ds(t * P, rows), :], y[0:rows, slot, :]
                                     ).then_inc(n_stored[slot], DMA)

                if l:
                    all_nodes_stored(sp, l - 1)
                sweep(sp, NODE_TILES, NODE_RING, -2, 2, move_nodes)
            all_nodes_stored(sp, LAYERS - 1)

        @block.gpsimd
        def _(pool):
            def triangle(buf, compare, sign=1):
                nc.gpsimd.affine_select(out=buf[:], in_=ones[:], compare_op=compare, fill=0.0, base=0,
                                        pattern=[[sign, P]], channel_multiplier=-sign).then_inc(consts, 1)

            nc.gpsimd.memset(dst_i[:], PAD_NODE).then_inc(pads_done, 1)
            nc.gpsimd.memset(src_i[:], 0).then_inc(pads_done, 1)
            nc.gpsimd.memset(ones[:], 1.0).then_inc(memset_done, 1)
            pool.wait_ge(memset_done, 1)
            triangle(ident, ALU.is_equal)
            triangle(below, ALU.is_gt, -1)
            triangle(above, ALU.is_gt)
            triangle(upto, ALU.is_ge)
            nc.gpsimd.iota(column_no[:], pattern=[[1, P]], base=0, channel_multiplier=0,
                           allow_small_or_imprecise_dtypes=True).then_inc(consts, 1)
            nc.gpsimd.iota(partition_no[:], pattern=[[1, 1]], base=0, channel_multiplier=1,
                           allow_small_or_imprecise_dtypes=True).then_inc(consts, 1)
            nc.gpsimd.memset(eps[:], EPS).then_inc(consts, 1)
            nc.gpsimd.memset(x_tile[:], 0.0).then_inc(consts, 1)
            nc.gpsimd.memset(residual[:], 0.0).then_inc(consts, 1)

            pool.wait_ge(records_ready, 1)

            def scatter(j, s, alive):
                t = j * EDGE_RING + s
                if not isinstance(j, int) or j > 0:
                    pool.wait_ge(scattered[s], j * DMA)
                nc.gpsimd.tensor_copy(scatter_rank[:, s:s + 1], rank_i[:, bass.ds(t, 1)]
                                      ).then_inc(scatter_copied, 1)
                nc.gpsimd.tensor_copy(scatter_record[:, s, :], record[:, bass.ds(t, 1), :]
                                      .rearrange("p a c -> p (a c)")).then_inc(scatter_copied, 1)
                pool.drain()
                nc.gpsimd.indirect_dma_start(
                    out=edge_records, out_offset=bass.IndirectOffsetOnAxis(ap=scatter_rank[:, s:s + 1], axis=0),
                    in_=scatter_record[:, s, :], in_offset=None).then_inc(scattered[s], DMA)

            for s in range(EDGE_RING):
                scatter(0, s, None)
            with pool.Fori(1, EDGE_TILES // EDGE_RING) as j:
                for s in range(EDGE_RING):
                    scatter(j, s, None)

            pool.wait_ge(sorted_ready, 1)
            for l in range(LAYERS):
                ph = edges(l)
                if l:
                    all_nodes_stored(pool, l - 1)

                def gather_sources(j, s, alive):
                    t, slot, turn = ph.at(j, s, 0)
                    reach(pool, e_turned, ph.tiles(t - EDGE_RING))
                    nc.gpsimd.tensor_copy(gather_idx[:, slot:slot + 1], sorted_src[:, bass.ds(t, 1)]
                                          ).then_inc(e_idx, 1)
                    pool.drain()
                    nc.gpsimd.indirect_dma_start(
                        out=gathered[:, slot, :], out_offset=None, in_=x_in if l == 0 else node_x,
                        in_offset=bass.IndirectOffsetOnAxis(ap=gather_idx[:, slot:slot + 1], axis=0)
                    ).then_inc(e_gathered[slot], DMA)

                for s in range(EDGE_RING):
                    gather_sources(0, s, None)
                with pool.Fori(1, EDGE_TILES // EDGE_RING) as j:
                    for s in range(EDGE_RING):
                        gather_sources(j, s, None)

                ph = nodes(l)
                if l == 0:
                    pool.wait_ge(owner_ready, 1)
                all_edge_rows_stored(pool, l)
                pool.wait_ge(bias_stored, DMA * (l + 1))

                def gather_edge_rows(j, s, alive):
                    t, slot, turn = ph.at(j, s, 0)
                    reach(pool, n_summed, ph.tiles(t - NODE_RING))
                    nc.gpsimd.tensor_copy(owner_idx[:, slot:slot + 1], owner[:, bass.ds(t, 1)]
                                          ).then_inc(n_idx, 1)
                    pool.drain()
                    nc.gpsimd.indirect_dma_start(
                        out=edge_row[:, slot, :], out_offset=None, in_=edge_table,
                        in_offset=bass.IndirectOffsetOnAxis(ap=owner_idx[:, slot:slot + 1], axis=0)
                    ).then_inc(n_gathered[slot], DMA)

                for s in range(NODE_RING):
                    gather_edge_rows(0, s, None)
                with pool.Fori(1, NODE_TILES // NODE_RING) as j:
                    for s in range(NODE_RING):
                        gather_edge_rows(j, s, None)
                for t in range(NODE_TILES // NODE_RING * NODE_RING, NODE_TILES):
                    gather_edge_rows(t // NODE_RING, t % NODE_RING, None)

        @block.tensor
        def _(pe):
            def split_product(psum, a_high, a_low, m):
                for k in range(K):
                    nc.tensor.matmul(psum, a_low[:, k, :], w_high[m][:, k, :], start=(k == 0), stop=False)
                    nc.tensor.matmul(psum, a_high[:, k, :], w_low[m][:, k, :], start=False, stop=False)
                    last = nc.tensor.matmul(psum, a_high[:, k, :], w_high[m][:, k, :],
                                            start=False, stop=(k == K - 1))
                return last

            def shift_product(m, of, l):
                pe.wait_ge(shift_done, l)
                pe.wait_ge(w_loaded[of], DMA * (l + 1))
                if l > 1:
                    pe.wait_ge(bias_done[m], l)
                for k in range(K):
                    last = nc.tensor.matmul(bank[6 if m == "p" else 7][:], shift_cols[:, k, :],
                                            stage[of][:, k, :], start=(k == 0), stop=(k == K - 1))
                last.then_inc(bias_product[m], 1)

            pe.wait_ge(consts, 9)

            def count_tile(j, s, first, last):
                t = j * EDGE_RING + s
                pe.wait_ge(hot_done, t + 1)
                nc.tensor.matmul(bank[0][:, 0:P], hot_lo_b[:, s, :], hot_hi_b[:, s, :],
                                 start=first, stop=last, skip_group_check=True)
                nc.tensor.matmul(bank[1][:, 0:P], hot_hi_b[:, s, :], hot_lo_b[:, s, :],
                                 start=first, stop=last, skip_group_check=True).then_inc(counted, 1)

            for s in range(EDGE_RING):
                count_tile(0, s, s == 0, False)
            with pe.Fori(1, EDGE_TILES // EDGE_RING - 1) as j:
                for s in range(EDGE_RING):
                    count_tile(j, s, False, False)
            for s in range(EDGE_RING):
                count_tile(EDGE_TILES // EDGE_RING - 1, s, False, s == EDGE_RING - 1)

            pe.wait_ge(prep, 2)
            nc.tensor.matmul(bank[2][:, 0:P], above[:], table[:, 1, :], start=True, stop=True
                             ).then_inc(prep_pe, 1)
            nc.tensor.matmul(bank[3][:, 0:P], count_lh[:], above[:], start=True, stop=True
                             ).then_inc(prep_pe, 1)
            pe.wait_ge(prep, 6)
            nc.tensor.matmul(bank[4][:, 0:P], upto[:], count_lh[:], start=True, stop=False)
            nc.tensor.matmul(bank[4][:, 0:P], total_cols[:], above[:], start=False, stop=True
                             ).then_inc(prep_pe, 1)
            nc.tensor.matmul(bank[5][:, 0:P], ident[:], start[:], start=True, stop=False,
                             skip_group_check=True).then_inc(table_added, 1)

            def rank_tile(j, s, first):
                t = j * EDGE_RING + s
                pe.wait_ge(diag_done, t + 1)
                if not first:
                    pe.wait_ge(in_tile_done, t - 1)
                nc.tensor.matmul(bank[s][:, 0:2 * P], ones[:], diag[:, s, :, :].rearrange("p a b -> p (a b)"),
                                 start=True, stop=True).then_inc(row_done, 1)
                pe.wait_ge(hot_t_done, t + 1)
                pe.wait_ge(table_copied, t + 1)
                if not first:
                    pe.wait_ge(rank_read, t - 1)
                nc.tensor.matmul(bank[2 + s][:, 0:2 * P], hot_t[:, s, :],
                                 table[:].rearrange("p a b -> p (a b)"), start=True, stop=True
                                 ).then_inc(looked_up, 1)
                pe.wait_ge(hot2_done, t + 1)
                nc.tensor.matmul(bank[5][:, 0:P], hot_hi_b[:, s, :], hot_lo_b[:, s, :], start=False,
                                 stop=False, skip_group_check=True).then_inc(table_added, 1)

            for s in range(EDGE_RING):
                rank_tile(0, s, True)
            with pe.Fori(1, EDGE_TILES // EDGE_RING) as j:
                for s in range(EDGE_RING):
                    rank_tile(j, s, False)

            def spread_tile(j, s, first):
                t = j * EDGE_RING + s
                pe.wait_ge(sdiag_done, t + 1)
                if not first:
                    pe.wait_ge(srow_copied, t - 1)
                nc.tensor.matmul(bank[6 + s][:, 0:P], ones[:], diag[:, s, 0, :], start=True, stop=True
                                 ).then_inc(srow_done, 1)

            for s in range(EDGE_RING):
                spread_tile(0, s, True)
            with pe.Fori(1, EDGE_TILES // EDGE_RING) as j:
                for s in range(EDGE_RING):
                    spread_tile(j, s, False)

            for l in range(LAYERS):
                ph = edges(l)
                if l:
                    shift_product("l", "r", l)
                for m in "pl":
                    pe.wait_ge(w_low_done[m], l + 1)

                def edge_step(j, s, alive):
                    if alive(1):
                        t, slot, turn = ph.at(j, s, 1)
                        if l == 0:
                            pe.wait_ge(in_s_done, t + 1)
                        else:
                            pe.wait_ge(e_gathered[slot], ph.slot(slot, turn))
                        reach(pe, e_xt_low, ph.tiles(t - EDGE_RING))
                        for k in range(K):
                            last = nc.tensor.transpose(bank[slot][:, k * P:(k + 1) * P],
                                                       gathered[:, slot, k * P:(k + 1) * P], ident[:])
                        last.then_inc(e_turned, 1)
                    if alive(-2):
                        t, slot, turn = ph.at(j, s, -2)
                        pe.wait_ge(e_agg_low, ph.tiles(t))
                        reach(pe, e_out, ph.tiles(t - EDGE_RING))
                        split_product(bank[6 + slot][:], agg_high, agg_low, "l").then_inc(e_product, 1)
                    if alive(-1):
                        t, slot, turn = ph.at(j, s, -1)
                        pe.wait_ge(e_masks, ph.tiles(t))
                        pe.wait_ge(e_h_low, ph.tiles(t))
                        reach(pe, e_agg, ph.tiles(t - EDGE_RING))
                        for k in range(K):
                            cols = slice(k * P, (k + 1) * P)
                            nc.tensor.matmul(bank[4 + slot][:, cols], h_low[:, cols], same[:, slot, :],
                                             start=True, stop=False)
                            last = nc.tensor.matmul(bank[4 + slot][:, cols], h_high[:, cols],
                                                    same[:, slot, :], start=False, stop=True)
                        last.then_inc(e_summed, 1)
                    if alive(0):
                        t, slot, turn = ph.at(j, s, 0)
                        pe.wait_ge(e_xt_low, ph.tiles(t))
                        reach(pe, e_h_pre, ph.tiles(t - EDGE_RING))
                        split_product(bank[2 + slot][:], xt_high[:, slot], xt_low[:, slot], "p"
                                      ).then_inc(e_projected, 1)

                sweep(pe, EDGE_TILES, EDGE_RING, -2, 1, edge_step)

                if l + 1 < LAYERS:
                    pe.wait_ge(e_out, EDGE_TILES * (l + 1))
                    shift_product("p", "p", l + 1)
                ph = nodes(l)
                pe.wait_ge(w_low_done["r"], l + 1)

                def node_step(j, s, alive):
                    if alive(1):
                        t, slot, turn = ph.at(j, s, 1)
                        if l == 0:
                            pe.wait_ge(in_s_done, t + (EDGE_TILES + 1))
                        else:
                            pe.wait_ge(n_loaded[slot], ph.slot(slot, turn))
                        reach(pe, n_xt_low, ph.tiles(t - NODE_RING))
                        for k in range(K):
                            last = nc.tensor.transpose(bank[slot][:, k * P:(k + 1) * P],
                                                       x_tile[:, slot, k * P:(k + 1) * P], ident[:])
                        last.then_inc(n_turned, 1)
                    if alive(0):
                        t, slot, turn = ph.at(j, s, 0)
                        pe.wait_ge(n_xt_low, ph.tiles(t))
                        reach(pe, n_summed, ph.tiles(t - NODE_RING))
                        split_product(bank[3 + slot][:], xt_high[:, slot], xt_low[:, slot], "r"
                                      ).then_inc(n_product, 1)

                sweep(pe, NODE_TILES, NODE_RING, 0, 1, node_step)

        @block.scalar
        def _(act):
            act.wait_ge(consts, 9)

            def high_of(m, l):
                act.wait_ge(w_loaded[m], DMA * (l + 1))
                if l and m != "l":
                    act.wait_ge(affine_loaded, 2 * DMA * l)
                    for k in range(K):
                        last = nc.scalar.activation(w_high[m][:, k, :], stage[m][:, k, :], ACT.Identity,
                                                    scale=gain[:, k:k + 1])
                else:
                    last = nc.scalar.activation(w_high[m][:], stage[m][:], ACT.Identity)
                last.then_inc(w_high_done[m], 1)

            high_of("p", 0)
            high_of("l", 0)

            def copy_table(t):
                act.wait_ge(table_added, t + 1)
                if not isinstance(t, int) or t > 0:
                    act.wait_ge(looked_up, t)
                nc.scalar.activation(table[:, 0, :], bank[5][:, 0:P], ACT.Identity).then_inc(table_copied, 1)

            copy_table(0)
            with act.Fori(1, EDGE_TILES) as t:
                copy_table(t)

            def copy_row(t, bank_no):
                act.wait_ge(srow_done, t + 1)
                nc.scalar.activation(dst_row[:, bass.ds(t * P + 1, P)], bank[bank_no][:, 0:P], ACT.Identity
                                     ).then_inc(srow_copied, 1)

            with act.Fori(0, EDGE_TILES // EDGE_RING) as j:
                for s in range(EDGE_RING):
                    copy_row(j * EDGE_RING + s, 6 + s)

            def in_std_of(t, base, slot):
                act.wait_ge(in_s_mean, t + (base + 1))
                nc.scalar.activation(in_std[:, slot:slot + 1], in_mean[:, slot, 1:2], ACT.Sqrt,
                                     bias=eps[:]).then_inc(in_s_std, 1)

            def in_norm(t, base, slot, buf):
                act.wait_ge(in_s_off, t + (base + 1))
                nc.scalar.activation(buf[:, slot, :], buf[:, slot, :], ACT.Identity,
                                     bias=in_off[:, slot:slot + 1], scale=in_rstd[:, slot:slot + 1]
                                     ).then_inc(in_s_done, 1)

            for l in range(LAYERS):
                if l:
                    act.wait_ge(n_product, NODE_TILES * l)
                high_of("r", l)
                ph = edges(l)
                turned_act = ACT.Relu if l == 0 else ACT.Identity

                def edge_step(j, s, alive):
                    if l == 0 and alive(2):
                        t, slot, turn = ph.at(j, s, 2)
                        in_std_of(t, 0, slot)
                    if alive(1):
                        t, slot, turn = ph.at(j, s, 1)
                        act.wait_ge(e_turned, ph.tiles(t))
                        reach(act, e_projected, ph.tiles(t - EDGE_RING))
                        nc.scalar.activation(xt_high[:, slot].rearrange("p k m -> p (k m)"), bank[slot][:],
                                             turned_act).then_inc(e_xt_high, 1)
                    if alive(-1):
                        t, slot, turn = ph.at(j, s, -1)
                        act.wait_ge(e_agg, ph.tiles(t))
                        reach(act, e_product, ph.tiles(t - 1))
                        nc.scalar.activation(agg_high[:], agg[:, slot], ACT.Identity).then_inc(e_agg_high, 1)
                    if alive(0):
                        t, slot, turn = ph.at(j, s, 0)
                        act.wait_ge(e_h_pre, ph.tiles(t))
                        reach(act, e_summed, ph.tiles(t - 1))
                        nc.scalar.activation(h_high[:], h_pre[:], ACT.Relu).then_inc(e_h_high, 1)
                    if l == 0 and alive(2):
                        t, slot, turn = ph.at(j, s, 2)
                        in_norm(t, 0, slot, gathered)

                sweep(act, EDGE_TILES, EDGE_RING, -1, 2 if l == 0 else 1, edge_step)

                act.wait_ge(e_projected, EDGE_TILES * (l + 1))
                act.wait_ge(e_product, EDGE_TILES * (l + 1))
                if l + 1 < LAYERS:
                    high_of("p", l + 1)
                    high_of("l", l + 1)
                ph = nodes(l)

                def node_step(j, s, alive):
                    if l == 0 and alive(2):
                        t, slot, turn = ph.at(j, s, 2)
                        in_std_of(t, EDGE_TILES, slot)
                    if alive(1):
                        t, slot, turn = ph.at(j, s, 1)
                        act.wait_ge(n_turned, ph.tiles(t))
                        reach(act, n_product, ph.tiles(t - NODE_RING))
                        nc.scalar.activation(xt_high[:, slot].rearrange("p k m -> p (k m)"), bank[slot][:],
                                             turned_act).then_inc(n_xt_high, 1)
                    if l + 1 < LAYERS:
                        if alive(-1):
                            t, slot, turn = ph.at(j, s, -1)
                            act.wait_ge(n_mean, ph.tiles(t))
                            nc.scalar.activation(ln_std[:, slot:slot + 1], ln_mean[:, slot, 1:2], ACT.Sqrt,
                                                 bias=eps[:]).then_inc(n_std, 1)
                        if alive(0):
                            t, slot, turn = ph.at(j, s, 0)
                            act.wait_ge(n_summed, ph.tiles(t))
                            nc.scalar.activation(y[:, slot, :], y[:, slot, :], ACT.Relu).then_inc(n_relu, 1)
                    if l == 0 and alive(2):
                        t, slot, turn = ph.at(j, s, 2)
                        in_norm(t, EDGE_TILES, slot, x_tile)

                sweep(act, NODE_TILES, NODE_RING, -1 if l + 1 < LAYERS else 0, 2 if l == 0 else 1, node_step)

        @block.vector
        def _(dve):
            V = nc.vector
            dve.wait_ge(consts, 9)
            V.memset(dst_row[:, 0:1], -1.0).then_inc(digits, 1)

            def low_of(m, l):
                dve.wait_ge(w_high_done[m], l + 1)
                if l and m != "l":
                    for k in range(K):
                        last = V.scalar_tensor_tensor(
                            out=w_low[m][:, k, :], in0=stage[m][:, k, :], scalar=gain[:, k:k + 1],
                            in1=w_high[m][:, k, :].bitcast(F32), op0=ALU.mult, op1=ALU.subtract)
                else:
                    last = V.tensor_tensor(w_low[m][:], stage[m][:], w_high[m][:].bitcast(F32), ALU.subtract)
                last.then_inc(w_low_done[m], 1)

            def shifted_bias(m, l):
                dve.wait_ge(bias_loaded[m], DMA * (l + 1))
                if l:
                    dve.wait_ge(bias_product[m], l)
                    V.tensor_tensor(bias[m][:], bank[6 if m == "p" else 7][:], bias_stage[m][:], ALU.add
                                    ).then_inc(bias_done[m], 1)
                else:
                    V.tensor_copy(bias[m][:], bias_stage[m][:]).then_inc(bias_done[m], 1)

            dve.wait_ge(graph_loaded, 2 * DMA)
            V.tensor_scalar(hi_i[:], dst_i[:], 7, None, ALU.arith_shift_right).then_inc(digits, 1)
            V.tensor_scalar(lo_i[:], dst_i[:], 127, None, ALU.bitwise_and).then_inc(digits, 1)
            V.tensor_copy(dst_f[:], dst_i[:]).then_inc(digits, 1)
            dve.wait_ge(digits, 4)
            V.tensor_copy(hi_f[:], hi_i[:]).then_inc(digits, 1)
            V.tensor_copy(lo_f[:], lo_i[:]).then_inc(digits, 1)
            dve.wait_ge(digits, 6)

            def hot(j, s, first):
                t = j * EDGE_RING + s
                if not first:
                    dve.wait_ge(counted, t - 1)
                V.tensor_scalar(hot_hi_b[:, s, :], column_no[:], hi_f[:, bass.ds(t, 1)], None, ALU.is_equal)
                V.tensor_scalar(hot_lo_b[:, s, :], column_no[:], lo_f[:, bass.ds(t, 1)], None, ALU.is_equal
                                ).then_inc(hot_done, 1)

            for s in range(EDGE_RING):
                hot(0, s, True)
            with dve.Fori(1, EDGE_TILES // EDGE_RING) as j:
                for s in range(EDGE_RING):
                    hot(j, s, False)

            dve.wait_ge(counted, EDGE_TILES)
            V.tensor_copy(count_lh[:], bank[0][:, 0:P]).then_inc(prep, 1)
            V.tensor_copy(table[:, 1, :], bank[1][:, 0:P]).then_inc(prep, 1)
            dve.wait_ge(prep_pe, 2)
            dve.wait_ge(prep, 2)
            V.tensor_reduce(tile_start[:], bank[2][:, 0:P], mybir.AxisListType.X, ALU.add).then_inc(prep, 1)
            V.tensor_reduce(column_total[:], table[:, 1, :], mybir.AxisListType.X, ALU.add).then_inc(prep, 1)
            dve.wait_ge(prep, 4)
            V.tensor_scalar(start[:], bank[3][:, 0:P], tile_start[:], None, ALU.add).then_inc(prep, 1)
            V.tensor_scalar(total_cols[:], ones[:], column_total[:], None, ALU.mult).then_inc(prep, 1)
            dve.wait_ge(prep_pe, 3)
            V.tensor_scalar(has_edges[:], count_lh[:], 0.0, None, ALU.is_gt).then_inc(prep, 1)
            V.tensor_scalar(owner_f[:], bank[4][:, 0:P], -1.0 - BIAS_ROW, None, ALU.add).then_inc(prep, 1)
            dve.wait_ge(prep, 8)
            V.tensor_tensor(owner_f2[:], owner_f[:], has_edges[:], ALU.mult).then_inc(prep, 1)
            dve.wait_ge(prep, 9)
            V.tensor_scalar(owner[:], owner_f2[:], float(BIAS_ROW), None, ALU.add).then_inc(owner_ready, 1)

            def rank(j, s, first):
                t = j * EDGE_RING + s
                col = bass.ds(t, 1)
                if not first:
                    dve.wait_ge(row_done, t - 1)
                    dve.wait_ge(table_added, t)
                    dve.wait_ge(rank_read, t - 1)
                V.tensor_scalar(diag[:, s, 0, :], ident[:], dst_f[:, col], None, ALU.mult)
                V.tensor_scalar(diag[:, s, 1, :], ident[:], hi_f[:, col], None, ALU.mult).then_inc(diag_done, 1)
                V.tensor_scalar(hot_hi_b[:, s, :], column_no[:], hi_f[:, col], None, ALU.is_equal)
                V.tensor_scalar(hot_lo_b[:, s, :], column_no[:], lo_f[:, col], None, ALU.is_equal)
                V.tensor_scalar(hot_lo[:, s, :], column_no[:], lo_f[:, col], None, ALU.is_equal
                                ).then_inc(hot2_done, 1)
                dve.wait_ge(row_done, t + 1)
                if not first:
                    dve.wait_ge(looked_up, t - 1)
                V.tensor_scalar(hot_t[:, s, :], bank[s][:, P:2 * P], partition_no[:], None, ALU.is_equal
                                ).then_inc(hot_t_done, 1)
                V.scalar_tensor_tensor(out=scratch[:], in0=bank[s][:, 0:P], scalar=dst_f[:, col],
                                       in1=below[:], op0=ALU.is_equal, op1=ALU.mult,
                                       accum_out=rank_in_tile[:, col]).then_inc(in_tile_done, 1)
                dve.wait_ge(looked_up, t + 1)
                dve.wait_ge(hot2_done, t + 1)
                dve.wait_ge(in_tile_done, t + 1)
                V.scalar_tensor_tensor(out=scratch[:], in0=bank[2 + s][:, 0:P], scalar=1.0,
                                       in1=hot_lo[:, s, :], op0=ALU.mult, op1=ALU.mult,
                                       accum_out=rank_start[:, col])
                V.scalar_tensor_tensor(out=scratch2[:], in0=bank[2 + s][:, P:2 * P], scalar=1.0,
                                       in1=hot_lo[:, s, :], op0=ALU.mult, op1=ALU.mult,
                                       accum_out=edge_count[:, col]).then_inc(rank_read, 1)

            for s in range(EDGE_RING):
                rank(0, s, True)
            with dve.Fori(1, EDGE_TILES // EDGE_RING) as j:
                for s in range(EDGE_RING):
                    rank(j, s, False)

            dve.wait_ge(rank_read, EDGE_TILES)
            V.tensor_tensor(rank_f[:], rank_start[:], rank_in_tile[:], ALU.add).then_inc(prep, 1)
            V.memset(record[:], 0.0).then_inc(prep, 1)
            dve.wait_ge(prep, 11)
            V.tensor_copy(rank_i[:], rank_f[:]).then_inc(prep, 1)
            V.tensor_copy(record[:, :, 0], src_i[:]).then_inc(prep, 1)
            V.tensor_copy(record[:, :, 1], dst_f[:]).then_inc(prep, 1)
            V.reciprocal(record[:, :, 2], edge_count[:]).then_inc(prep, 1)
            dve.wait_ge(prep, 15)
            V.tensor_copy(scratch[:, 0:1], scratch2[:, 0:1]).then_inc(records_ready, 1)

            for m in "pl":
                low_of(m, 0)
                shifted_bias(m, 0)

            dve.wait_ge(sorted_loaded, DMA)
            V.tensor_copy(sorted_src[:], sorted_record[:, :, 0]).then_inc(sorted_ready, 1)

            def spread(j, s, first):
                t = j * EDGE_RING + s
                if not first:
                    dve.wait_ge(srow_done, t - 1)
                V.tensor_scalar(diag[:, s, 0, :], ident[:],
                                sorted_record[:, bass.ds(t, 1), 1:2].rearrange("p a c -> p (a c)"), None,
                                ALU.mult).then_inc(sdiag_done, 1)

            for s in range(EDGE_RING):
                spread(0, s, True)
            with dve.Fori(1, EDGE_TILES // EDGE_RING) as j:
                for s in range(EDGE_RING):
                    spread(j, s, False)
            dve.wait_ge(srow_copied, EDGE_TILES)

            def in_moments(t, base, slot, buf, loaded, value):
                dve.wait_ge(loaded, value)
                V.bn_stats(in_stats[:, slot, :], buf[:, slot, :]).then_inc(in_s_stats, 1)
                dve.drain()
                V.bn_aggr(in_mean[:, slot, :], in_stats[:, slot, :]).then_inc(in_s_mean, 1)

            def in_scale(t, base, slot):
                dve.wait_ge(in_s_std, t + (base + 1))
                V.reciprocal(in_rstd[:, slot:slot + 1], in_std[:, slot:slot + 1]).then_inc(in_s_rstd, 1)
                dve.wait_ge(in_s_rstd, t + (base + 1))
                V.scalar_tensor_tensor(out=in_off[:, slot:slot + 1], in0=in_mean[:, slot, 0:1], scalar=-1.0,
                                       in1=in_rstd[:, slot:slot + 1], op0=ALU.mult, op1=ALU.mult
                                       ).then_inc(in_s_off, 1)

            def xt_low_of(l, slot):
                turned = bank[slot][:]
                high = xt_high[:, slot].rearrange("p k m -> p (k m)").bitcast(F32)
                low = xt_low[:, slot].rearrange("p k m -> p (k m)")
                if l == 0:
                    return V.scalar_tensor_tensor(out=low, in0=turned, scalar=0.0, in1=high,
                                                  op0=ALU.max, op1=ALU.subtract)
                return V.tensor_tensor(low, turned, high, ALU.subtract)

            for l in range(LAYERS):
                low_of("r", l)
                if l:
                    shifted_bias("l", l)
                ph = edges(l)

                def edge_step(j, s, alive):
                    if l == 0 and alive(2):
                        t, slot, turn = ph.at(j, s, 2)
                        in_moments(t, 0, slot, gathered, e_gathered[slot], ph.slot(slot, turn))
                    if alive(0):
                        t, slot, turn = ph.at(j, s, 0)
                        reach(dve, e_summed, ph.tiles(t - EDGE_RING))
                        row = dst_row[:, bass.ds(t * P + 1, P)]
                        V.tensor_scalar(same[:, slot, :], row,
                                        sorted_record[:, bass.ds(t, 1), 1:2].rearrange("p a c -> p (a c)"),
                                        None, ALU.is_equal)
                        V.tensor_scalar(carries[:, slot, :], row, dst_row[:, bass.ds(t * P, 1)], None,
                                        ALU.is_equal).then_inc(e_masks, 1)
                    if alive(1):
                        t, slot, turn = ph.at(j, s, 1)
                        dve.wait_ge(e_xt_high, ph.tiles(t))
                        xt_low_of(l, slot).then_inc(e_xt_low, 1)
                    if alive(-2):
                        t, slot, turn = ph.at(j, s, -2)
                        dve.wait_ge(e_product, ph.tiles(t))
                        reach(dve, e_stored[slot], ph.slot(slot, turn - 1))
                        V.scalar_tensor_tensor(
                            out=edge_out[:, slot, :], in0=bank[6 + slot][:],
                            scalar=sorted_record[:, bass.ds(t, 1), 2:3].rearrange("p a c -> p (a c)"),
                            in1=bias["l"][:], op0=ALU.mult, op1=ALU.add).then_inc(e_out, 1)
                    if alive(-1):
                        t, slot, turn = ph.at(j, s, -1)
                        dve.wait_ge(e_summed, ph.tiles(t))
                        if isinstance(t, int) and t == 0:
                            V.tensor_copy(agg[:, slot].rearrange("p k m -> p (k m)"), bank[4 + slot][:]
                                          ).then_inc(e_agg, 1)
                        else:
                            dve.wait_ge(e_agg, ph.tiles(t - 1))
                            dve.wait_ge(e_masks, ph.tiles(t))
                            for k in range(K):
                                last = V.scalar_tensor_tensor(
                                    out=agg[:, slot, k, :], in0=carries[:, slot, :],
                                    scalar=agg[:, 1 - slot, k, P - 1:P],
                                    in1=bank[4 + slot][:, k * P:(k + 1) * P], op0=ALU.mult, op1=ALU.add)
                            last.then_inc(e_agg, 1)
                        dve.wait_ge(e_agg_high, ph.tiles(t))
                        V.tensor_tensor(agg_low[:], agg[:, slot], agg_high[:].bitcast(F32), ALU.subtract
                                        ).then_inc(e_agg_low, 1)
                    if alive(0):
                        t, slot, turn = ph.at(j, s, 0)
                        dve.wait_ge(e_projected, ph.tiles(t))
                        reach(dve, e_h_low, ph.tiles(t - 1))
                        V.tensor_tensor(h_pre[:], bank[2 + slot][:], bias["p"][:], ALU.add
                                        ).then_inc(e_h_pre, 1)
                        dve.wait_ge(e_h_high, ph.tiles(t))
                        V.scalar_tensor_tensor(out=h_low[:], in0=h_pre[:], scalar=0.0,
                                               in1=h_high[:].bitcast(F32), op0=ALU.max, op1=ALU.subtract
                                               ).then_inc(e_h_low, 1)
                    if l == 0 and alive(2):
                        t, slot, turn = ph.at(j, s, 2)
                        in_scale(t, 0, slot)

                sweep(dve, EDGE_TILES, EDGE_RING, -2, 2 if l == 0 else 1, edge_step)

                if l + 1 < LAYERS:
                    dve.wait_ge(affine_loaded, 2 * DMA * (l + 1))
                    for k in range(K):
                        last = V.tensor_scalar(shift_cols[:, k, :], ones[:], shift[:, k:k + 1], None, ALU.mult)
                    last.then_inc(shift_done, 1)
                    low_of("p", l + 1)
                    low_of("l", l + 1)
                    shifted_bias("p", l + 1)
                ph = nodes(l)

                def node_step(j, s, alive):
                    if l == 0 and alive(2):
                        t, slot, turn = ph.at(j, s, 2)
                        in_moments(t, EDGE_TILES, slot, x_tile, n_loaded[slot], ph.slot(slot, turn))
                    if alive(1):
                        t, slot, turn = ph.at(j, s, 1)
                        dve.wait_ge(n_xt_high, ph.tiles(t))
                        xt_low_of(l, slot).then_inc(n_xt_low, 1)
                    if l + 1 < LAYERS and alive(-1):
                        t, slot, turn = ph.at(j, s, -1)
                        dve.wait_ge(n_relu, ph.tiles(t))
                        V.bn_stats(ln_stats[:, slot, :], y[:, slot, :]).then_inc(n_stats, 1)
                        dve.drain()
                        V.bn_aggr(ln_mean[:, slot, :], ln_stats[:, slot, :]).then_inc(n_mean, 1)
                    if alive(0):
                        t, slot, turn = ph.at(j, s, 0)
                        dve.wait_ge(n_product, ph.tiles(t))
                        dve.wait_ge(n_gathered[slot], ph.slot(slot, turn))
                        reach(dve, n_stored[slot], ph.slot(slot, turn - 1))
                        V.tensor_tensor(y[:, slot, :], bank[3 + slot][:], edge_row[:, slot, :], ALU.add
                                        ).then_inc(n_summed, 1)
                        if l == LAYERS - 1:
                            dve.wait_ge(n_summed, ph.tiles(t))
                            last_layer = Phase(0, NODE_TILES, NODE_RING)
                            dve.wait_ge(n_residual[slot], last_layer.slot(slot, turn))
                            V.tensor_tensor(y[:, slot, :], y[:, slot, :], residual[:, slot, :], ALU.add
                                            ).then_inc(n_out, 1)
                    if l + 1 < LAYERS and alive(-1):
                        t, slot, turn = ph.at(j, s, -1)
                        dve.wait_ge(n_std, ph.tiles(t))
                        V.reciprocal(ln_rstd[:, slot:slot + 1], ln_std[:, slot:slot + 1]).then_inc(n_rstd, 1)
                        dve.wait_ge(n_rstd, ph.tiles(t))
                        V.tensor_scalar(y[:, slot, :], y[:, slot, :], ln_mean[:, slot, 0:1],
                                        ln_rstd[:, slot:slot + 1], ALU.subtract, ALU.mult).then_inc(n_out, 1)
                    if l == 0 and alive(2):
                        t, slot, turn = ph.at(j, s, 2)
                        in_scale(t, EDGE_TILES, slot)

                sweep(dve, NODE_TILES, NODE_RING, -1 if l + 1 < LAYERS else 0, 2 if l == 0 else 1, node_step)


def kernel(**inputs):
    import numpy as np
    import concourse.bacc as bacc
    from concourse.bass_utils import run_bass_kernel_spmd

    nc = bacc.Bacc("TRN2", target_bir_lowering=False, num_devices=1)
    arrays = {}

    def given(name, a):
        a = np.ascontiguousarray(a)
        arrays[name] = a
        return nc.dram_tensor(name, a.shape, mybir.dt.from_np(a.dtype), kind="ExternalInput").ap()

    x = given("x", inputs["x"])
    src = given("src", inputs["src"])
    dst = given("dst", inputs["dst"])
    weights = []
    for l in range(LAYERS):
        w = {}
        for m in "plr":
            w["W" + m] = given(f"W{m}{l}_t", np.asarray(inputs[f"L0_gnn_W{m}{l}"]).T)
        for m in "pl":
            w["b" + m] = given(f"b{m}{l}", inputs[f"L0_gnn_b{m}{l}"])
        if l:
            for name in ("g", "be"):
                column = np.asarray(inputs[f"L0_gnn_{name}{l - 1}"]).reshape(-1, P).T
                w[name] = given(f"{name}{l - 1}", column)
        weights.append(w)
    out = nc.dram_tensor("out", arrays["x"].shape, F32, kind="ExternalOutput").ap()
    sage_kernel(nc, x, src, dst, weights, out)
    r = run_bass_kernel_spmd(nc, [arrays], core_ids=[0])
    return r.results[0]["out"]
```

```python
from contextlib import ExitStack

import concourse.bass as bass
from concourse import mybir

P = 128
ALU = mybir.AluOpType
ACT = mybir.ActivationFunctionType
F32 = mybir.dt.float32
F32R = mybir.dt.float32r
BF16 = mybir.dt.bfloat16
I32 = mybir.dt.int32
EPS = 1e-5
LAYERS = 3
CONSTS = 12
DMA = 16
EDGE_RING = 2
NODE_RING = 3


def sweep(eng, count, ring, low, high, body):
    first, end = 1 - low // ring, (count - high) // ring

    def written_out(i):
        body(i // ring, i % ring, lambda d: 0 <= i + d < count)

    for i in range(-high, first * ring):
        written_out(i)
    with eng.Fori(first, end) as j:
        for s in range(ring):
            body(j, s, lambda d: True)
    for i in range(end * ring, count - low):
        written_out(i)


def sage_kernel(nc, x_in, src_in, dst_in, weights, out):
    N, D = x_in.shape
    E = src_in.shape[0]
    K = D // P
    NODE_TILES = -(-N // P)
    LAST_ROWS = N - (NODE_TILES - 1) * P
    EDGE_TILES = -(-E // P)
    EDGES = EDGE_TILES * P
    EDGE_ROWS = E // EDGE_TILES
    PAD_NODE = NODE_TILES * P
    BIAS_ROW = EDGES
    assert D == 512 and EDGE_ROWS * EDGE_TILES == E and EDGE_ROWS <= P and NODE_TILES < P

    with ExitStack() as ctx:
        def sb(name, shape, dt):
            return ctx.enter_context(nc.sbuf_tensor(name, shape, dt))

        def sem(name):
            return ctx.enter_context(nc.semaphore(name))

        def sems(name, n):
            return [sem(f"{name}{i}") for i in range(n)]

        node_x = nc.dram_tensor("node_x", [NODE_TILES * P, D], F32).ap()
        edge_table = nc.dram_tensor("edge_table", [EDGES + 1, D], F32).ap()
        edge_records = nc.dram_tensor("edge_records", [EDGES, 4], F32).ap()

        bank = [ctx.enter_context(nc.psum_tensor(f"bank{i}", [P, 512], F32)) for i in range(8)]

        stage = {m: sb(f"stage_{m}", [P, K, D], F32) for m in "plr"}
        w_high = {m: sb(f"w_high_{m}", [P, K, D], F32R) for m in "plr"}
        w_low = {m: sb(f"w_low_{m}", [P, K, D], F32R) for m in "plr"}
        bias_stage = {m: sb(f"bias_stage_{m}", [P, D], F32) for m in "pl"}
        bias = {m: sb(f"bias_{m}", [P, D], F32) for m in "pl"}
        gain = sb("gain", [P, K], F32)
        shift = sb("shift", [P, K], F32)
        shift_cols = sb("shift_cols", [P, K, P], F32)

        ones = sb("ones", [P, P], F32)
        ident = sb("ident", [P, P], F32)
        below = sb("below", [P, P], F32)
        above = sb("above", [P, P], F32)
        upto = sb("upto", [P, P], F32)
        column_no = sb("column_no", [P, P], F32)
        partition_no = sb("partition_no", [P, 1], F32)
        eps = sb("eps", [P, 1], F32)
        ones_b = sb("ones_b", [P, P], BF16)
        digit_b = sb("digit_b", [P, P], BF16)
        ident_b = sb("ident_b", [P, P], BF16)

        dst_i = sb("dst_i", [P, EDGE_TILES], I32)
        src_i = sb("src_i", [P, EDGE_TILES], I32)
        hi_i = sb("hi_i", [P, EDGE_TILES], I32)
        lo_i = sb("lo_i", [P, EDGE_TILES], I32)
        dst_f = sb("dst_f", [P, EDGE_TILES], F32)
        hi_f = sb("hi_f", [P, EDGE_TILES], F32)
        lo_f = sb("lo_f", [P, EDGE_TILES], F32)
        hot_hi_b = sb("hot_hi_b", [P, EDGE_RING, P], BF16)
        hot_lo_b = sb("hot_lo_b", [P, EDGE_RING, P], BF16)
        diag_hi = sb("diag_hi", [P, EDGE_RING, P], BF16)
        diag_lo = sb("diag_lo", [P, EDGE_RING, P], BF16)
        hot_t = sb("hot_t", [P, EDGE_RING, P], F32)
        count_lh = sb("count_lh", [P, P], F32)
        table = sb("table", [P, 2, P], F32)
        start = sb("start", [P, P], F32)
        column_total = sb("column_total", [P, 1], F32)
        tile_start = sb("tile_start", [P, 1], F32)
        total_cols = sb("total_cols", [P, P], F32)
        unused = sb("unused", [P, 3, EDGE_RING, P], F32)
        rank_start = sb("rank_start", [P, EDGE_TILES], F32)
        rank_in_tile = sb("rank_in_tile", [P, EDGE_TILES], F32)
        rank_i = sb("rank_i", [P, EDGE_TILES], I32)
        edge_count = sb("edge_count", [P, EDGE_TILES], F32)
        record = sb("record", [P, EDGE_TILES, 4], F32)
        scatter_rank = sb("scatter_rank", [P, EDGE_RING], I32)
        scatter_record = sb("scatter_record", [P, EDGE_RING, 4], F32)
        sorted_record = sb("sorted_record", [P, EDGE_TILES, 4], F32)
        sorted_dst = sb("sorted_dst", [P, EDGE_TILES], F32)
        sorted_src = sb("sorted_src", [P, EDGE_TILES], I32)
        dst_row = sb("dst_row", [P, 1 + EDGES], F32)
        has_edges = sb("has_edges", [P, P], F32)
        owner_f = sb("owner_f", [P, P], F32)
        owner_f2 = sb("owner_f2", [P, P], F32)
        owner = sb("owner", [P, P], I32)

        gathered = sb("gathered", [P, EDGE_RING, D], F32)
        gather_idx = sb("gather_idx", [P, EDGE_RING], I32)
        same = sb("same", [P, EDGE_RING, P], F32R)
        carries = sb("carries", [P, EDGE_RING, P], F32)
        h_pre = sb("h_pre", [P, D], F32)
        h_high = sb("h_high", [P, D], F32R)
        h_low = sb("h_low", [P, D], F32R)
        agg = sb("agg", [P, EDGE_RING, K, P], F32)
        agg_high = sb("agg_high", [P, K, P], F32R)
        agg_low = sb("agg_low", [P, K, P], F32R)
        edge_out = sb("edge_out", [P, EDGE_RING, D], F32)

        xt_high = sb("xt_high", [P, NODE_RING, K, P], F32R)
        xt_low = sb("xt_low", [P, NODE_RING, K, P], F32R)

        x_tile = sb("x_tile", [P, NODE_RING, D], F32)
        residual = sb("residual", [P, NODE_RING, D], F32)
        owner_idx = sb("owner_idx", [P, NODE_RING], I32)
        edge_row = sb("edge_row", [P, NODE_RING, D], F32)
        y = sb("y", [P, NODE_RING, D], F32)

        in_stats = sb("in_stats", [P, NODE_RING, 6], F32)
        in_mean = sb("in_mean", [P, NODE_RING, 2], F32)
        in_std = sb("in_std", [P, NODE_RING], F32)
        in_rstd = sb("in_rstd", [P, NODE_RING], F32)
        in_off = sb("in_off", [P, NODE_RING], F32)
        ln_stats = sb("ln_stats", [P, NODE_RING, 6], F32)
        ln_mean = sb("ln_mean", [P, NODE_RING, 2], F32)
        ln_std = sb("ln_std", [P, NODE_RING], F32)
        ln_rstd = sb("ln_rstd", [P, NODE_RING], F32)

        w_loaded = {m: sem(f"w_loaded_{m}") for m in "plr"}
        bias_loaded = {m: sem(f"bias_loaded_{m}") for m in "pl"}
        affine_loaded = sem("affine_loaded")
        w_high_done = {m: sem(f"w_high_done_{m}") for m in "plr"}
        w_low_done = {m: sem(f"w_low_done_{m}") for m in "plr"}
        shift_done = sem("shift_done")
        bias_product = {m: sem(f"bias_product_{m}") for m in "pl"}
        bias_done = {m: sem(f"bias_done_{m}") for m in "pl"}
        bias_stored = sem("bias_stored")

        consts = sem("consts")
        memset_done = sem("memset_done")
        pads_done = sem("pads_done")
        graph_loaded = sem("graph_loaded")
        digits = sem("digits")
        hot_done = sem("hot_done")
        counted = sem("counted")
        prep = sem("prep")
        prep_pe = sem("prep_pe")
        diag_done = sem("diag_done")
        row_done = sem("row_done")
        hot_t_done = sem("hot_t_done")
        hot2_done = sem("hot2_done")
        in_tile_done = sem("in_tile_done")
        table_copied = sem("table_copied")
        table_added = sem("table_added")
        looked_up = sem("looked_up")
        rank_read = sem("rank_read")
        ranked = sem("ranked")
        sorted_dst_ready = sem("sorted_dst_ready")
        scatter_copied = sem("scatter_copied")
        scattered = sems("scattered", EDGE_RING)
        sorted_loaded = sem("sorted_loaded")
        sorted_ready = sem("sorted_ready")
        sdiag_done = sem("sdiag_done")
        srow_done = sem("srow_done")
        srow_copied = sem("srow_copied")
        owner_ready = sem("owner_ready")

        e_idx = sem("e_idx")
        e_gathered = sems("e_gathered", EDGE_RING)
        e_turned = sem("e_turned")
        e_xt_high = sem("e_xt_high")
        e_xt_low = sem("e_xt_low")
        e_projected = sem("e_projected")
        e_h_pre = sem("e_h_pre")
        e_h_high = sem("e_h_high")
        e_h_low = sem("e_h_low")
        e_masks = sem("e_masks")
        e_summed = sem("e_summed")
        e_agg = sem("e_agg")
        e_agg_high = sem("e_agg_high")
        e_agg_low = sem("e_agg_low")
        e_product = sem("e_product")
        e_out = sem("e_out")
        e_stored = sems("e_stored", EDGE_RING)

        n_loaded = sems("n_loaded", NODE_RING)
        n_residual = sems("n_residual", NODE_RING)
        n_idx = sem("n_idx")
        n_gathered = sems("n_gathered", NODE_RING)
        n_turned = sem("n_turned")
        n_xt_high = sem("n_xt_high")
        n_xt_low = sem("n_xt_low")
        n_product = sem("n_product")
        n_summed = sem("n_summed")
        n_relu = sem("n_relu")
        n_stats = sem("n_stats")
        n_mean = sem("n_mean")
        n_std = sem("n_std")
        n_rstd = sem("n_rstd")
        n_out = sem("n_out")
        n_stored = sems("n_stored", NODE_RING)

        in_s_stats = sem("in_s_stats")
        in_s_mean = sem("in_s_mean")
        in_s_std = sem("in_s_std")
        in_s_rstd = sem("in_s_rstd")
        in_s_off = sem("in_s_off")
        in_s_done = sem("in_s_done")

        def reach(eng, s, value):
            if not isinstance(value, int) or value > 0:
                eng.wait_ge(s, value)

        class Phase:

            def __init__(self, l, count, ring):
                self.l, self.count, self.ring = l, count, ring

            def at(self, j, s, d):
                return j * self.ring + (s + d), (s + d) % self.ring, j + (s + d) // self.ring

            def tiles(self, t):
                return t + (self.l * self.count + 1)

            def slot(self, slot, turn):
                per_layer = -(-(self.count - slot) // self.ring)
                return turn * DMA + (self.l * per_layer + 1) * DMA

        def edges(l):
            return Phase(l, EDGE_TILES, EDGE_RING)

        def nodes(l):
            return Phase(l, NODE_TILES, NODE_RING)

        def all_edge_rows_stored(eng, l):
            for s in range(EDGE_RING):
                eng.wait_ge(e_stored[s], DMA * (l + 1) * (-(-(EDGE_TILES - s) // EDGE_RING)))

        def all_nodes_stored(eng, l):
            for s in range(NODE_RING):
                eng.wait_ge(n_stored[s], DMA * (l + 1) * (-(-(NODE_TILES - s) // NODE_RING)))

        block = ctx.enter_context(nc.Block())

        @block.sync
        def _(sp):
            def load_weights(l, ms):
                for m in ms:
                    if l:
                        sp.wait_ge(w_low_done[m], l)
                        sp.wait_ge(w_high_done[m], l)
                        if l > 1 and m == "p":
                            sp.wait_ge(bias_product["p"], l - 1)
                        if l > 1 and m == "r":
                            sp.wait_ge(bias_product["l"], l - 1)
                    sp.dma_start(stage[m][:], weights[l]["W" + m].rearrange("(k p) n -> p k n", p=P)
                                 ).then_inc(w_loaded[m], DMA)

            def load_biases(l):
                for m in "pl":
                    if l:
                        sp.wait_ge(bias_done[m], l)
                    sp.dma_start(bias_stage[m][:], weights[l]["b" + m].rearrange("(a n) -> a n", a=1)
                                 .to_broadcast([P, D])).then_inc(bias_loaded[m], DMA)

            def load_affine(l):
                if l > 1:
                    sp.wait_ge(w_low_done["r"], l)
                    sp.wait_ge(w_high_done["r"], l)
                    sp.wait_ge(w_low_done["p"], l)
                    sp.wait_ge(shift_done, l - 1)
                for buf, name in ((gain, "g"), (shift, "be")):
                    sp.dma_start(buf[:], weights[l][name]).then_inc(affine_loaded, DMA)

            sp.wait_ge(pads_done, 2)
            sp.dma_start(dst_i[0:EDGE_ROWS, :], dst_in.rearrange("(p t) -> p t", t=EDGE_TILES)
                         ).then_inc(graph_loaded, DMA)
            sp.dma_start(src_i[0:EDGE_ROWS, :], src_in.rearrange("(p t) -> p t", t=EDGE_TILES)
                         ).then_inc(graph_loaded, DMA)
            load_weights(0, "plr")
            load_biases(0)
            for s in range(EDGE_RING):
                sp.wait_ge(scattered[s], DMA * EDGE_TILES // EDGE_RING)
            sp.dma_start(sorted_record[:], edge_records.rearrange("(t p) c -> p t c", p=P)
                         ).then_inc(sorted_loaded, DMA)

            for l in range(LAYERS):
                if l + 1 < LAYERS:
                    load_affine(l + 1)
                    load_weights(l + 1, "pl")
                sp.wait_ge(bias_done["l"], l + 1)
                sp.dma_start(edge_table[BIAS_ROW:BIAS_ROW + 1, :], bias["l"][0:1, :]
                             ).then_inc(bias_stored, DMA)
                ph = edges(l)

                def store_edges(j, s, alive):
                    t, slot, turn = ph.at(j, s, 0)
                    sp.wait_ge(e_out, ph.tiles(t))
                    sp.dma_start(edge_table[bass.ds(t * P, P), :], edge_out[:, slot, :]
                                 ).then_inc(e_stored[slot], DMA)

                sweep(sp, EDGE_TILES, EDGE_RING, 0, 0, store_edges)

                if l + 1 < LAYERS:
                    load_biases(l + 1)
                    load_weights(l + 1, "r")
                ph = nodes(l)
                source = x_in if l == 0 else node_x
                target = out if l == LAYERS - 1 else node_x

                def move_nodes(j, s, alive):
                    if alive(3):
                        t, slot, turn = ph.at(j, s, 3)
                        rows = P if not isinstance(t, int) or t < NODE_TILES - 1 or l else LAST_ROWS
                        reach(sp, n_turned, ph.tiles(t - NODE_RING))
                        sp.dma_start(x_tile[0:rows, slot, :], source[bass.ds(t * P, rows), :]
                                     ).then_inc(n_loaded[slot], DMA)
                        if l == LAYERS - 1:
                            rows = P if not isinstance(t, int) or t < NODE_TILES - 1 else LAST_ROWS
                            if not isinstance(t, int) or t >= NODE_RING:
                                sp.wait_ge(n_out, ph.tiles(t - NODE_RING))
                            sp.dma_start(residual[0:rows, slot, :], x_in[bass.ds(t * P, rows), :]
                                         ).then_inc(n_residual[slot], DMA)
                    if alive(-1):
                        t, slot, turn = ph.at(j, s, -1)
                        last = isinstance(t, int) and t == NODE_TILES - 1 and l == LAYERS - 1
                        rows = LAST_ROWS if last else P
                        sp.wait_ge(n_out, ph.tiles(t))
                        sp.dma_start(target[bass.ds(t * P, rows), :], y[0:rows, slot, :]
                                     ).then_inc(n_stored[slot], DMA)

                if l:
                    all_nodes_stored(sp, l - 1)
                sweep(sp, NODE_TILES, NODE_RING, -1, 3, move_nodes)
            all_nodes_stored(sp, LAYERS - 1)

        @block.gpsimd
        def _(pool):
            def triangle(buf, compare, sign=1):
                nc.gpsimd.affine_select(out=buf[:], in_=ones[:], compare_op=compare, fill=0.0, base=0,
                                        pattern=[[sign, P]], channel_multiplier=-sign).then_inc(consts, 1)

            nc.gpsimd.memset(dst_i[:], PAD_NODE).then_inc(pads_done, 1)
            nc.gpsimd.memset(src_i[:], 0).then_inc(pads_done, 1)
            nc.gpsimd.memset(ones[:], 1.0).then_inc(memset_done, 1)
            pool.wait_ge(memset_done, 1)
            triangle(ident, ALU.is_equal)
            triangle(below, ALU.is_gt, -1)
            triangle(above, ALU.is_gt)
            triangle(upto, ALU.is_ge)
            nc.gpsimd.iota(column_no[:], pattern=[[1, P]], base=0, channel_multiplier=0,
                           allow_small_or_imprecise_dtypes=True).then_inc(consts, 1)
            nc.gpsimd.iota(partition_no[:], pattern=[[1, 1]], base=0, channel_multiplier=1,
                           allow_small_or_imprecise_dtypes=True).then_inc(consts, 1)
            nc.gpsimd.memset(eps[:], EPS).then_inc(consts, 1)
            nc.gpsimd.memset(ones_b[:], 1.0).then_inc(consts, 1)
            nc.gpsimd.memset(digit_b[:], float(P)).then_inc(consts, 1)
            nc.gpsimd.memset(ident_b[:], 0.0).then_inc(memset_done, 1)
            pool.wait_ge(memset_done, 2)
            nc.gpsimd.affine_select(out=ident_b[:], in_=ident_b[:], compare_op=ALU.not_equal, fill=1.0, base=0,
                                    pattern=[[1, P]], channel_multiplier=-1).then_inc(consts, 1)
            nc.gpsimd.memset(x_tile[:], 0.0).then_inc(consts, 1)
            nc.gpsimd.memset(residual[:], 0.0).then_inc(consts, 1)


            def indexed(count, ring, copy, issue):
                copy(0, 0, 0, True)
                groups = count // ring
                for s in range(ring):
                    copy((s + 1) // ring, (s + 1) % ring, s + 1, False)
                    issue(0, s, s)
                with pool.Fori(1, groups - 1) as j:
                    for s in range(ring):
                        copy(j + (s + 1) // ring, (s + 1) % ring, j * ring + (s + 1), False)
                        issue(j, s, j * ring + s)
                for t in range((groups - 1) * ring, count):
                    if t + 1 < count:
                        copy((t + 1) // ring, (t + 1) % ring, t + 1, False)
                    else:
                        copy(None, None, count, False)
                    issue(t // ring, t % ring, t)

            def copy_record(j, s, t, first):
                if j is None:
                    pool.wait_ge(scatter_copied, 2 * t)
                    return
                if not first:
                    pool.wait_ge(scatter_copied, t * 2)
                if not isinstance(j, int) or j > 0:
                    pool.wait_ge(scattered[s], j * DMA)
                pool.wait_ge(ranked, t * 2 + 2)
                nc.gpsimd.tensor_copy(scatter_rank[:, s:s + 1], rank_i[:, bass.ds(t, 1)]
                                      ).then_inc(scatter_copied, 1)
                nc.gpsimd.tensor_copy(scatter_record[:, s, :], record[:, bass.ds(t, 1), :]
                                      .rearrange("p a c -> p (a c)")).then_inc(scatter_copied, 1)

            def scatter(j, s, t):
                nc.gpsimd.indirect_dma_start(
                    out=edge_records, out_offset=bass.IndirectOffsetOnAxis(ap=scatter_rank[:, s:s + 1], axis=0),
                    in_=scatter_record[:, s, :], in_offset=None).then_inc(scattered[s], DMA)

            indexed(EDGE_TILES, EDGE_RING, copy_record, scatter)

            pool.wait_ge(sorted_ready, 1)
            for l in range(LAYERS):
                ph = edges(l)
                if l:
                    all_nodes_stored(pool, l - 1)

                def copy_index(ph, idx_copied, gathers, freed, idx_buf, table):
                    def copy(j, s, t, first):
                        if not first:
                            pool.wait_ge(idx_copied, ph.tiles(t - 1))
                            reach(pool, freed, ph.tiles(t - 1 - ph.ring))
                        if j is None:
                            return
                        reach(pool, gathers[s], ph.slot(s, j - 1))
                        nc.gpsimd.tensor_copy(idx_buf[:, s:s + 1], table[:, bass.ds(t, 1)]
                                              ).then_inc(idx_copied, 1)
                    return copy

                def gather_sources(j, s, t):
                    nc.gpsimd.indirect_dma_start(
                        out=gathered[:, s, :], out_offset=None, in_=x_in if l == 0 else node_x,
                        in_offset=bass.IndirectOffsetOnAxis(ap=gather_idx[:, s:s + 1], axis=0)
                    ).then_inc(e_gathered[s], DMA)

                indexed(EDGE_TILES, EDGE_RING,
                        copy_index(ph, e_idx, e_gathered, e_turned, gather_idx, sorted_src), gather_sources)

                ph = nodes(l)
                if l == 0:
                    pool.wait_ge(owner_ready, 1)
                all_edge_rows_stored(pool, l)
                pool.wait_ge(bias_stored, DMA * (l + 1))

                def gather_edge_rows(j, s, t):
                    nc.gpsimd.indirect_dma_start(
                        out=edge_row[:, s, :], out_offset=None, in_=edge_table,
                        in_offset=bass.IndirectOffsetOnAxis(ap=owner_idx[:, s:s + 1], axis=0)
                    ).then_inc(n_gathered[s], DMA)

                indexed(NODE_TILES, NODE_RING,
                        copy_index(ph, n_idx, n_gathered, n_summed, owner_idx, owner), gather_edge_rows)

        @block.tensor
        def _(pe):
            def split_product(psum, a_high, a_low, m):
                for k in range(K):
                    nc.tensor.matmul(psum, a_low[:, k, :], w_high[m][:, k, :], start=(k == 0), stop=False)
                    nc.tensor.matmul(psum, a_high[:, k, :], w_low[m][:, k, :], start=False, stop=False)
                    last = nc.tensor.matmul(psum, a_high[:, k, :], w_high[m][:, k, :],
                                            start=False, stop=(k == K - 1))
                return last

            def shift_product(m, of, l):
                pe.wait_ge(shift_done, l)
                pe.wait_ge(w_loaded[of], DMA * (l + 1))
                if l > 1:
                    pe.wait_ge(bias_done[m], l)
                for k in range(K):
                    last = nc.tensor.matmul(bank[6 if m == "p" else 7][:], shift_cols[:, k, :],
                                            stage[of][:, k, :], start=(k == 0), stop=(k == K - 1))
                last.then_inc(bias_product[m], 1)

            pe.wait_ge(consts, CONSTS)

            def count_tile(j, s, first, last):
                t = j * EDGE_RING + s
                pe.wait_ge(hot_done, t + 1)
                nc.tensor.matmul(bank[0][:, 0:P], hot_lo_b[:, s, :], hot_hi_b[:, s, :],
                                 start=first, stop=last, skip_group_check=True)
                nc.tensor.matmul(bank[1][:, 0:P], hot_hi_b[:, s, :], hot_lo_b[:, s, :],
                                 start=first, stop=last, skip_group_check=True).then_inc(counted, 1)

            for s in range(EDGE_RING):
                count_tile(0, s, s == 0, False)
            with pe.Fori(1, EDGE_TILES // EDGE_RING - 1) as j:
                for s in range(EDGE_RING):
                    count_tile(j, s, False, False)
            for s in range(EDGE_RING):
                count_tile(EDGE_TILES // EDGE_RING - 1, s, False, s == EDGE_RING - 1)

            pe.wait_ge(prep, 2)
            nc.tensor.matmul(bank[2][:, 0:P], above[:], table[:, 1, :], start=True, stop=True
                             ).then_inc(prep_pe, 1)
            nc.tensor.matmul(bank[3][:, 0:P], count_lh[:], above[:], start=True, stop=True
                             ).then_inc(prep_pe, 1)
            pe.wait_ge(prep, 6)
            nc.tensor.matmul(bank[4][:, 0:P], upto[:], count_lh[:], start=True, stop=False)
            nc.tensor.matmul(bank[4][:, 0:P], total_cols[:], above[:], start=False, stop=True
                             ).then_inc(prep_pe, 1)
            nc.tensor.matmul(bank[5][:, 0:P], ident[:], start[:], start=True, stop=False,
                             skip_group_check=True).then_inc(table_added, 1)

            def rank_step(j, s, alive):
                if alive(1):
                    t, slot = j * EDGE_RING + (s + 1), (s + 1) % EDGE_RING
                    pe.wait_ge(diag_done, t + 1)
                    reach(pe, in_tile_done, t - 1)
                    nc.tensor.matmul(bank[slot][:, 0:P], ones_b[:], diag_lo[:, slot, :], start=True, stop=False)
                    nc.tensor.matmul(bank[slot][:, 0:P], digit_b[:], diag_hi[:, slot, :], start=False, stop=True)
                    nc.tensor.matmul(bank[slot][:, P:2 * P], ones_b[:], diag_hi[:, slot, :], start=True,
                                     stop=True).then_inc(row_done, 1)
                if alive(0):
                    t, slot = j * EDGE_RING + s, s
                    pe.wait_ge(hot_t_done, t + 1)
                    pe.wait_ge(table_copied, t + 1)
                    reach(pe, rank_read, t - 1)
                    nc.tensor.matmul(bank[2 + slot][:, 0:2 * P], hot_t[:, slot, :],
                                     table[:].rearrange("p a b -> p (a b)"), start=True, stop=True
                                     ).then_inc(looked_up, 1)
                    nc.tensor.matmul(bank[5][:, 0:P], hot_hi_b[:, slot, :], hot_lo_b[:, slot, :], start=False,
                                     stop=False, skip_group_check=True).then_inc(table_added, 1)

            sweep(pe, EDGE_TILES, EDGE_RING, 0, 1, rank_step)

            def spread_tile(j, s, first):
                t = j * EDGE_RING + s
                pe.wait_ge(sdiag_done, t + 1)
                if not first:
                    pe.wait_ge(srow_copied, t - 1)
                nc.tensor.matmul(bank[6 + s][:, 0:P], ones_b[:], diag_lo[:, s, :], start=True, stop=False)
                nc.tensor.matmul(bank[6 + s][:, 0:P], digit_b[:], diag_hi[:, s, :], start=False, stop=True
                                 ).then_inc(srow_done, 1)

            for s in range(EDGE_RING):
                spread_tile(0, s, True)
            with pe.Fori(1, EDGE_TILES // EDGE_RING) as j:
                for s in range(EDGE_RING):
                    spread_tile(j, s, False)

            for l in range(LAYERS):
                ph = edges(l)
                if l:
                    shift_product("l", "r", l)
                for m in "pl":
                    pe.wait_ge(w_low_done[m], l + 1)

                def edge_step(j, s, alive):
                    if alive(1):
                        t, slot, turn = ph.at(j, s, 1)
                        if l == 0:
                            pe.wait_ge(in_s_done, t + 1)
                        else:
                            pe.wait_ge(e_gathered[slot], ph.slot(slot, turn))
                        reach(pe, e_xt_low, ph.tiles(t - EDGE_RING))
                        for k in range(K):
                            last = nc.tensor.transpose(bank[slot][:, k * P:(k + 1) * P],
                                                       gathered[:, slot, k * P:(k + 1) * P], ident[:])
                        last.then_inc(e_turned, 1)
                    if alive(-2):
                        t, slot, turn = ph.at(j, s, -2)
                        pe.wait_ge(e_agg_low, ph.tiles(t))
                        reach(pe, e_out, ph.tiles(t - EDGE_RING))
                        split_product(bank[6 + slot][:], agg_high, agg_low, "l").then_inc(e_product, 1)
                    if alive(-1):
                        t, slot, turn = ph.at(j, s, -1)
                        pe.wait_ge(e_masks, ph.tiles(t))
                        pe.wait_ge(e_h_low, ph.tiles(t))
                        reach(pe, e_agg, ph.tiles(t - EDGE_RING))
                        for k in range(K):
                            cols = slice(k * P, (k + 1) * P)
                            nc.tensor.matmul(bank[4 + slot][:, cols], h_low[:, cols], same[:, slot, :],
                                             start=True, stop=False)
                            last = nc.tensor.matmul(bank[4 + slot][:, cols], h_high[:, cols],
                                                    same[:, slot, :], start=False, stop=True)
                        last.then_inc(e_summed, 1)
                    if alive(0):
                        t, slot, turn = ph.at(j, s, 0)
                        pe.wait_ge(e_xt_low, ph.tiles(t))
                        reach(pe, e_h_pre, ph.tiles(t - EDGE_RING))
                        split_product(bank[2 + slot][:], xt_high[:, slot], xt_low[:, slot], "p"
                                      ).then_inc(e_projected, 1)

                sweep(pe, EDGE_TILES, EDGE_RING, -2, 1, edge_step)

                if l + 1 < LAYERS:
                    pe.wait_ge(e_out, EDGE_TILES * (l + 1))
                    shift_product("p", "p", l + 1)
                ph = nodes(l)
                pe.wait_ge(w_low_done["r"], l + 1)

                def node_step(j, s, alive):
                    if alive(1):
                        t, slot, turn = ph.at(j, s, 1)
                        if l == 0:
                            pe.wait_ge(in_s_done, t + (EDGE_TILES + 1))
                        else:
                            pe.wait_ge(n_loaded[slot], ph.slot(slot, turn))
                        reach(pe, n_xt_low, ph.tiles(t - NODE_RING))
                        for k in range(K):
                            last = nc.tensor.transpose(bank[slot][:, k * P:(k + 1) * P],
                                                       x_tile[:, slot, k * P:(k + 1) * P], ident[:])
                        last.then_inc(n_turned, 1)
                    if alive(0):
                        t, slot, turn = ph.at(j, s, 0)
                        pe.wait_ge(n_xt_low, ph.tiles(t))
                        reach(pe, n_summed, ph.tiles(t - NODE_RING))
                        split_product(bank[3 + slot][:], xt_high[:, slot], xt_low[:, slot], "r"
                                      ).then_inc(n_product, 1)

                sweep(pe, NODE_TILES, NODE_RING, 0, 1, node_step)

        @block.scalar
        def _(act):
            act.wait_ge(consts, CONSTS)

            def high_of(m, l):
                act.wait_ge(w_loaded[m], DMA * (l + 1))
                if l and m != "l":
                    act.wait_ge(affine_loaded, 2 * DMA * l)
                    for k in range(K):
                        last = nc.scalar.activation(w_high[m][:, k, :], stage[m][:, k, :], ACT.Identity,
                                                    scale=gain[:, k:k + 1])
                else:
                    last = nc.scalar.activation(w_high[m][:], stage[m][:], ACT.Identity)
                last.then_inc(w_high_done[m], 1)

            high_of("p", 0)
            high_of("l", 0)

            def copy_table(t):
                act.wait_ge(table_added, t + 1)
                if not isinstance(t, int) or t > 0:
                    act.wait_ge(looked_up, t)
                nc.scalar.activation(table[:, 0, :], bank[5][:, 0:P], ACT.Identity).then_inc(table_copied, 1)

            copy_table(0)
            with act.Fori(1, EDGE_TILES) as t:
                copy_table(t)

            def copy_row(t, bank_no):
                act.wait_ge(srow_done, t + 1)
                nc.scalar.activation(dst_row[:, bass.ds(t * P + 1, P)], bank[bank_no][:, 0:P], ACT.Identity
                                     ).then_inc(srow_copied, 1)

            with act.Fori(0, EDGE_TILES // EDGE_RING) as j:
                for s in range(EDGE_RING):
                    copy_row(j * EDGE_RING + s, 6 + s)

            def in_std_of(t, base, slot):
                act.wait_ge(in_s_mean, t + (base + 1))
                nc.scalar.activation(in_std[:, slot:slot + 1], in_mean[:, slot, 1:2], ACT.Sqrt,
                                     bias=eps[:]).then_inc(in_s_std, 1)

            def in_norm(t, base, slot, buf):
                act.wait_ge(in_s_off, t + (base + 1))
                nc.scalar.activation(buf[:, slot, :], buf[:, slot, :], ACT.Identity,
                                     bias=in_off[:, slot:slot + 1], scale=in_rstd[:, slot:slot + 1]
                                     ).then_inc(in_s_done, 1)

            for l in range(LAYERS):
                if l:
                    act.wait_ge(n_product, NODE_TILES * l)
                high_of("r", l)
                ph = edges(l)
                turned_act = ACT.Relu if l == 0 else ACT.Identity

                def edge_step(j, s, alive):
                    if l == 0 and alive(2):
                        t, slot, turn = ph.at(j, s, 2)
                        in_std_of(t, 0, slot)
                    if alive(1):
                        t, slot, turn = ph.at(j, s, 1)
                        act.wait_ge(e_turned, ph.tiles(t))
                        reach(act, e_projected, ph.tiles(t - EDGE_RING))
                        nc.scalar.activation(xt_high[:, slot].rearrange("p k m -> p (k m)"), bank[slot][:],
                                             turned_act).then_inc(e_xt_high, 1)
                    if l == 0 and alive(2):
                        t, slot, turn = ph.at(j, s, 2)
                        in_norm(t, 0, slot, gathered)
                    if alive(-1):
                        t, slot, turn = ph.at(j, s, -1)
                        act.wait_ge(e_agg, ph.tiles(t))
                        reach(act, e_product, ph.tiles(t - 1))
                        nc.scalar.activation(agg_high[:], agg[:, slot], ACT.Identity).then_inc(e_agg_high, 1)
                    if alive(0):
                        t, slot, turn = ph.at(j, s, 0)
                        act.wait_ge(e_h_pre, ph.tiles(t))
                        reach(act, e_summed, ph.tiles(t - 1))
                        nc.scalar.activation(h_high[:], h_pre[:], ACT.Relu).then_inc(e_h_high, 1)

                sweep(act, EDGE_TILES, EDGE_RING, -1, 2 if l == 0 else 1, edge_step)

                act.wait_ge(e_projected, EDGE_TILES * (l + 1))
                act.wait_ge(e_product, EDGE_TILES * (l + 1))
                if l + 1 < LAYERS:
                    high_of("p", l + 1)
                    high_of("l", l + 1)
                ph = nodes(l)

                def node_step(j, s, alive):
                    if l == 0 and alive(2):
                        t, slot, turn = ph.at(j, s, 2)
                        in_std_of(t, EDGE_TILES, slot)
                    if alive(1):
                        t, slot, turn = ph.at(j, s, 1)
                        act.wait_ge(n_turned, ph.tiles(t))
                        reach(act, n_product, ph.tiles(t - NODE_RING))
                        nc.scalar.activation(xt_high[:, slot].rearrange("p k m -> p (k m)"), bank[slot][:],
                                             turned_act).then_inc(n_xt_high, 1)
                    if l + 1 < LAYERS:
                        if alive(-1):
                            t, slot, turn = ph.at(j, s, -1)
                            act.wait_ge(n_mean, ph.tiles(t))
                            nc.scalar.activation(ln_std[:, slot:slot + 1], ln_mean[:, slot, 1:2], ACT.Sqrt,
                                                 bias=eps[:]).then_inc(n_std, 1)
                        if l == 0 and alive(2):
                            t, slot, turn = ph.at(j, s, 2)
                            in_norm(t, EDGE_TILES, slot, x_tile)
                        if alive(0):
                            t, slot, turn = ph.at(j, s, 0)
                            act.wait_ge(n_summed, ph.tiles(t))
                            nc.scalar.activation(y[:, slot, :], y[:, slot, :], ACT.Relu).then_inc(n_relu, 1)

                sweep(act, NODE_TILES, NODE_RING, -1 if l + 1 < LAYERS else 0, 2 if l == 0 else 1, node_step)

        @block.vector
        def _(dve):
            V = nc.vector
            dve.wait_ge(consts, CONSTS)
            V.memset(dst_row[:, 0:1], -1.0).then_inc(digits, 1)

            def low_of(m, l):
                dve.wait_ge(w_high_done[m], l + 1)
                if l and m != "l":
                    for k in range(K):
                        last = V.scalar_tensor_tensor(
                            out=w_low[m][:, k, :], in0=stage[m][:, k, :], scalar=gain[:, k:k + 1],
                            in1=w_high[m][:, k, :].bitcast(F32), op0=ALU.mult, op1=ALU.subtract)
                else:
                    last = V.tensor_tensor(w_low[m][:], stage[m][:], w_high[m][:].bitcast(F32), ALU.subtract)
                last.then_inc(w_low_done[m], 1)

            def shifted_bias(m, l):
                dve.wait_ge(bias_loaded[m], DMA * (l + 1))
                if l:
                    dve.wait_ge(bias_product[m], l)
                    V.tensor_tensor(bias[m][:], bank[6 if m == "p" else 7][:], bias_stage[m][:], ALU.add
                                    ).then_inc(bias_done[m], 1)
                else:
                    V.tensor_copy(bias[m][:], bias_stage[m][:]).then_inc(bias_done[m], 1)

            dve.wait_ge(graph_loaded, 2 * DMA)
            V.tensor_scalar(hi_i[:], dst_i[:], 7, None, ALU.arith_shift_right).then_inc(digits, 1)
            V.tensor_scalar(lo_i[:], dst_i[:], 127, None, ALU.bitwise_and).then_inc(digits, 1)
            V.tensor_copy(dst_f[:], dst_i[:]).then_inc(digits, 1)
            dve.wait_ge(digits, 4)
            V.tensor_copy(hi_f[:], hi_i[:]).then_inc(digits, 1)
            V.tensor_copy(lo_f[:], lo_i[:]).then_inc(digits, 1)
            dve.wait_ge(digits, 6)

            def hot(j, s, first):
                t = j * EDGE_RING + s
                if not first:
                    dve.wait_ge(counted, t - 1)
                V.tensor_scalar(hot_hi_b[:, s, :], column_no[:], hi_f[:, bass.ds(t, 1)], None, ALU.is_equal)
                V.tensor_scalar(hot_lo_b[:, s, :], column_no[:], lo_f[:, bass.ds(t, 1)], None, ALU.is_equal
                                ).then_inc(hot_done, 1)

            for s in range(EDGE_RING):
                hot(0, s, True)
            with dve.Fori(1, EDGE_TILES // EDGE_RING) as j:
                for s in range(EDGE_RING):
                    hot(j, s, False)

            dve.wait_ge(counted, EDGE_TILES)
            V.tensor_copy(count_lh[:], bank[0][:, 0:P]).then_inc(prep, 1)
            V.tensor_copy(table[:, 1, :], bank[1][:, 0:P]).then_inc(prep, 1)
            dve.wait_ge(prep_pe, 2)
            dve.wait_ge(prep, 2)
            V.tensor_reduce(tile_start[:], bank[2][:, 0:P], mybir.AxisListType.X, ALU.add).then_inc(prep, 1)
            V.tensor_reduce(column_total[:], table[:, 1, :], mybir.AxisListType.X, ALU.add).then_inc(prep, 1)
            dve.wait_ge(prep, 4)
            V.tensor_scalar(start[:], bank[3][:, 0:P], tile_start[:], None, ALU.add).then_inc(prep, 1)
            V.tensor_scalar(total_cols[:], ones[:], column_total[:], None, ALU.mult).then_inc(prep, 1)
            dve.wait_ge(prep_pe, 3)
            V.tensor_scalar(has_edges[:], count_lh[:], 0.0, None, ALU.is_gt).then_inc(prep, 1)
            V.tensor_scalar(owner_f[:], bank[4][:, 0:P], -1.0 - BIAS_ROW, None, ALU.add).then_inc(prep, 1)
            dve.wait_ge(prep, 8)
            V.tensor_tensor(owner_f2[:], owner_f[:], has_edges[:], ALU.mult).then_inc(prep, 1)
            dve.wait_ge(prep, 9)
            V.tensor_scalar(owner[:], owner_f2[:], float(BIAS_ROW), None, ALU.add).then_inc(owner_ready, 1)

            V.tensor_copy(record[:, :, 0], src_i[:]).then_inc(prep, 1)
            V.tensor_copy(record[:, :, 1], hi_f[:]).then_inc(prep, 1)
            V.tensor_copy(record[:, :, 2], lo_f[:]).then_inc(prep, 1)
            dve.wait_ge(prep, 12)

            def rank_step(j, s, alive):
                if alive(2):
                    t, slot = j * EDGE_RING + (s + 2), s
                    reach(dve, row_done, t - 1)
                    V.tensor_scalar(diag_hi[:, slot, :], ident_b[:], hi_f[:, bass.ds(t, 1)], None, ALU.mult)
                    V.tensor_scalar(diag_lo[:, slot, :], ident_b[:], lo_f[:, bass.ds(t, 1)], None, ALU.mult
                                    ).then_inc(diag_done, 1)
                if alive(1):
                    t, slot = j * EDGE_RING + (s + 1), (s + 1) % EDGE_RING
                    col = bass.ds(t, 1)
                    reach(dve, table_added, t)
                    reach(dve, rank_read, t - 1)
                    V.tensor_scalar(hot_hi_b[:, slot, :], column_no[:], hi_f[:, col], None, ALU.is_equal)
                    V.tensor_scalar(hot_lo_b[:, slot, :], column_no[:], lo_f[:, col], None, ALU.is_equal
                                    ).then_inc(hot2_done, 1)
                    dve.wait_ge(row_done, t + 1)
                    V.tensor_scalar(hot_t[:, slot, :], bank[slot][:, P:2 * P], partition_no[:], None,
                                    ALU.is_equal).then_inc(hot_t_done, 1)
                    V.scalar_tensor_tensor(out=unused[:, 0, slot, :], in0=bank[slot][:, 0:P], scalar=dst_f[:, col],
                                           in1=below[:], op0=ALU.is_equal, op1=ALU.mult,
                                           accum_out=rank_in_tile[:, col]).then_inc(in_tile_done, 1)
                if alive(0):
                    t, slot = j * EDGE_RING + s, s
                    col = bass.ds(t, 1)
                    dve.wait_ge(looked_up, t + 1)
                    dve.wait_ge(hot2_done, t + 1)
                    dve.wait_ge(in_tile_done, t + 1)
                    V.scalar_tensor_tensor(out=unused[:, 1, slot, :], in0=bank[2 + slot][:, 0:P], scalar=1.0,
                                           in1=hot_lo_b[:, slot, :], op0=ALU.mult, op1=ALU.mult,
                                           accum_out=rank_start[:, col])
                    V.scalar_tensor_tensor(out=unused[:, 2, slot, :], in0=bank[2 + slot][:, P:2 * P], scalar=1.0,
                                           in1=hot_lo_b[:, slot, :], op0=ALU.mult, op1=ALU.mult,
                                           accum_out=edge_count[:, col]).then_inc(rank_read, 1)
                    dve.wait_ge(rank_read, t + 1)
                    V.tensor_tensor(rank_i[:, col], rank_start[:, col], rank_in_tile[:, col], ALU.add
                                    ).then_inc(ranked, 1)
                    V.reciprocal(record[:, col, 3:4].rearrange("p a c -> p (a c)"), edge_count[:, col]
                                 ).then_inc(ranked, 1)

            sweep(dve, EDGE_TILES, EDGE_RING, 0, 2, rank_step)

            for m in "pl":
                low_of(m, 0)
                shifted_bias(m, 0)

            dve.wait_ge(sorted_loaded, DMA)
            V.tensor_copy(sorted_src[:], sorted_record[:, :, 0]).then_inc(sorted_ready, 1)
            V.scalar_tensor_tensor(out=sorted_dst[:], in0=sorted_record[:, :, 1], scalar=float(P),
                                   in1=sorted_record[:, :, 2], op0=ALU.mult, op1=ALU.add
                                   ).then_inc(sorted_dst_ready, 1)

            def spread(j, s, first):
                t = j * EDGE_RING + s
                if not first:
                    dve.wait_ge(srow_done, t - 1)
                for buf, digit in ((diag_hi, 1), (diag_lo, 2)):
                    last = V.tensor_scalar(
                        buf[:, s, :], ident_b[:],
                        sorted_record[:, bass.ds(t, 1), digit:digit + 1].rearrange("p a c -> p (a c)"),
                        None, ALU.mult)
                last.then_inc(sdiag_done, 1)

            for s in range(EDGE_RING):
                spread(0, s, True)
            with dve.Fori(1, EDGE_TILES // EDGE_RING) as j:
                for s in range(EDGE_RING):
                    spread(j, s, False)
            dve.wait_ge(srow_copied, EDGE_TILES)
            dve.wait_ge(sorted_dst_ready, 1)

            def in_moments(t, base, slot, buf, loaded, value):
                dve.wait_ge(loaded, value)
                V.bn_stats(in_stats[:, slot, :], buf[:, slot, :]).then_inc(in_s_stats, 1)
                dve.drain()
                V.bn_aggr(in_mean[:, slot, :], in_stats[:, slot, :]).then_inc(in_s_mean, 1)

            def in_scale(t, base, slot):
                dve.wait_ge(in_s_std, t + (base + 1))
                V.reciprocal(in_rstd[:, slot:slot + 1], in_std[:, slot:slot + 1]).then_inc(in_s_rstd, 1)
                dve.wait_ge(in_s_rstd, t + (base + 1))
                V.scalar_tensor_tensor(out=in_off[:, slot:slot + 1], in0=in_mean[:, slot, 0:1], scalar=-1.0,
                                       in1=in_rstd[:, slot:slot + 1], op0=ALU.mult, op1=ALU.mult
                                       ).then_inc(in_s_off, 1)

            def xt_low_of(l, slot):
                turned = bank[slot][:]
                high = xt_high[:, slot].rearrange("p k m -> p (k m)").bitcast(F32)
                low = xt_low[:, slot].rearrange("p k m -> p (k m)")
                if l == 0:
                    return V.scalar_tensor_tensor(out=low, in0=turned, scalar=0.0, in1=high,
                                                  op0=ALU.max, op1=ALU.subtract)
                return V.tensor_tensor(low, turned, high, ALU.subtract)

            for l in range(LAYERS):
                low_of("r", l)
                if l:
                    shifted_bias("l", l)
                ph = edges(l)

                def edge_step(j, s, alive):
                    if l == 0 and alive(2):
                        t, slot, turn = ph.at(j, s, 2)
                        in_moments(t, 0, slot, gathered, e_gathered[slot], ph.slot(slot, turn))
                    if alive(0):
                        t, slot, turn = ph.at(j, s, 0)
                        reach(dve, e_summed, ph.tiles(t - EDGE_RING))
                        row = dst_row[:, bass.ds(t * P + 1, P)]
                        V.tensor_scalar(same[:, slot, :], row, sorted_dst[:, bass.ds(t, 1)], None, ALU.is_equal)
                        V.tensor_scalar(carries[:, slot, :], row, dst_row[:, bass.ds(t * P, 1)], None,
                                        ALU.is_equal).then_inc(e_masks, 1)
                    if alive(1):
                        t, slot, turn = ph.at(j, s, 1)
                        dve.wait_ge(e_xt_high, ph.tiles(t))
                        xt_low_of(l, slot).then_inc(e_xt_low, 1)
                    if l == 0 and alive(2):
                        t, slot, turn = ph.at(j, s, 2)
                        in_scale(t, 0, slot)
                    if alive(-2):
                        t, slot, turn = ph.at(j, s, -2)
                        dve.wait_ge(e_product, ph.tiles(t))
                        reach(dve, e_stored[slot], ph.slot(slot, turn - 1))
                        V.scalar_tensor_tensor(
                            out=edge_out[:, slot, :], in0=bank[6 + slot][:],
                            scalar=sorted_record[:, bass.ds(t, 1), 3:4].rearrange("p a c -> p (a c)"),
                            in1=bias["l"][:], op0=ALU.mult, op1=ALU.add).then_inc(e_out, 1)
                    if alive(-1):
                        t, slot, turn = ph.at(j, s, -1)
                        dve.wait_ge(e_summed, ph.tiles(t))
                        if isinstance(t, int) and t == 0:
                            V.tensor_copy(agg[:, slot].rearrange("p k m -> p (k m)"), bank[4 + slot][:]
                                          ).then_inc(e_agg, 1)
                        else:
                            dve.wait_ge(e_agg, ph.tiles(t - 1))
                            dve.wait_ge(e_masks, ph.tiles(t))
                            for k in range(K):
                                last = V.scalar_tensor_tensor(
                                    out=agg[:, slot, k, :], in0=carries[:, slot, :],
                                    scalar=agg[:, 1 - slot, k, P - 1:P],
                                    in1=bank[4 + slot][:, k * P:(k + 1) * P], op0=ALU.mult, op1=ALU.add)
                            last.then_inc(e_agg, 1)
                        dve.wait_ge(e_agg_high, ph.tiles(t))
                        V.tensor_tensor(agg_low[:], agg[:, slot], agg_high[:].bitcast(F32), ALU.subtract
                                        ).then_inc(e_agg_low, 1)
                    if alive(0):
                        t, slot, turn = ph.at(j, s, 0)
                        dve.wait_ge(e_projected, ph.tiles(t))
                        reach(dve, e_h_low, ph.tiles(t - 1))
                        V.tensor_tensor(h_pre[:], bank[2 + slot][:], bias["p"][:], ALU.add
                                        ).then_inc(e_h_pre, 1)
                        dve.wait_ge(e_h_high, ph.tiles(t))
                        V.scalar_tensor_tensor(out=h_low[:], in0=h_pre[:], scalar=0.0,
                                               in1=h_high[:].bitcast(F32), op0=ALU.max, op1=ALU.subtract
                                               ).then_inc(e_h_low, 1)

                sweep(dve, EDGE_TILES, EDGE_RING, -2, 2 if l == 0 else 1, edge_step)

                if l + 1 < LAYERS:
                    dve.wait_ge(affine_loaded, 2 * DMA * (l + 1))
                    for k in range(K):
                        last = V.tensor_scalar(shift_cols[:, k, :], ones[:], shift[:, k:k + 1], None, ALU.mult)
                    last.then_inc(shift_done, 1)
                    low_of("p", l + 1)
                    low_of("l", l + 1)
                    shifted_bias("p", l + 1)
                ph = nodes(l)

                def node_step(j, s, alive):
                    if l == 0 and alive(2):
                        t, slot, turn = ph.at(j, s, 2)
                        in_moments(t, EDGE_TILES, slot, x_tile, n_loaded[slot], ph.slot(slot, turn))
                    if alive(1):
                        t, slot, turn = ph.at(j, s, 1)
                        dve.wait_ge(n_xt_high, ph.tiles(t))
                        xt_low_of(l, slot).then_inc(n_xt_low, 1)
                    if l + 1 < LAYERS and alive(-1):
                        t, slot, turn = ph.at(j, s, -1)
                        dve.wait_ge(n_relu, ph.tiles(t))
                        V.bn_stats(ln_stats[:, slot, :], y[:, slot, :]).then_inc(n_stats, 1)
                        dve.drain()
                        V.bn_aggr(ln_mean[:, slot, :], ln_stats[:, slot, :]).then_inc(n_mean, 1)
                    if l == 0 and alive(2):
                        t, slot, turn = ph.at(j, s, 2)
                        in_scale(t, EDGE_TILES, slot)
                    if l + 1 < LAYERS and alive(-1):
                        t, slot, turn = ph.at(j, s, -1)
                        dve.wait_ge(n_std, ph.tiles(t))
                        V.reciprocal(ln_rstd[:, slot:slot + 1], ln_std[:, slot:slot + 1]).then_inc(n_rstd, 1)
                        dve.wait_ge(n_rstd, ph.tiles(t))
                        V.tensor_scalar(y[:, slot, :], y[:, slot, :], ln_mean[:, slot, 0:1],
                                        ln_rstd[:, slot:slot + 1], ALU.subtract, ALU.mult).then_inc(n_out, 1)
                    if alive(0):
                        t, slot, turn = ph.at(j, s, 0)
                        dve.wait_ge(n_product, ph.tiles(t))
                        dve.wait_ge(n_gathered[slot], ph.slot(slot, turn))
                        reach(dve, n_stored[slot], ph.slot(slot, turn - 1))
                        V.tensor_tensor(y[:, slot, :], bank[3 + slot][:], edge_row[:, slot, :], ALU.add
                                        ).then_inc(n_summed, 1)
                        if l == LAYERS - 1:
                            dve.wait_ge(n_summed, ph.tiles(t))
                            last_layer = Phase(0, NODE_TILES, NODE_RING)
                            dve.wait_ge(n_residual[slot], last_layer.slot(slot, turn))
                            V.tensor_tensor(y[:, slot, :], y[:, slot, :], residual[:, slot, :], ALU.add
                                            ).then_inc(n_out, 1)

                sweep(dve, NODE_TILES, NODE_RING, -1 if l + 1 < LAYERS else 0, 2 if l == 0 else 1, node_step)


def kernel(**inputs):
    import numpy as np
    import concourse.bacc as bacc
    from concourse.bass_utils import run_bass_kernel_spmd

    nc = bacc.Bacc("TRN2", target_bir_lowering=False, num_devices=1)
    arrays = {}

    def given(name, a):
        a = np.ascontiguousarray(a)
        arrays[name] = a
        return nc.dram_tensor(name, a.shape, mybir.dt.from_np(a.dtype), kind="ExternalInput").ap()

    x = given("x", inputs["x"])
    src = given("src", inputs["src"])
    dst = given("dst", inputs["dst"])
    weights = []
    for l in range(LAYERS):
        w = {}
        for m in "plr":
            w["W" + m] = given(f"W{m}{l}_t", np.asarray(inputs[f"L0_gnn_W{m}{l}"]).T)
        for m in "pl":
            w["b" + m] = given(f"b{m}{l}", inputs[f"L0_gnn_b{m}{l}"])
        if l:
            for name in ("g", "be"):
                column = np.asarray(inputs[f"L0_gnn_{name}{l - 1}"]).reshape(-1, P).T
                w[name] = given(f"{name}{l - 1}", column)
        weights.append(w)
    out = nc.dram_tensor("out", arrays["x"].shape, F32, kind="ExternalOutput").ap()
    sage_kernel(nc, x, src, dst, weights, out)
    r = run_bass_kernel_spmd(nc, [arrays], core_ids=[0])
    return r.results[0]["out"]
```

```python
from contextlib import ExitStack

import concourse.bass as bass
from concourse import mybir

P = 128
ALU = mybir.AluOpType
ACT = mybir.ActivationFunctionType
F32 = mybir.dt.float32
F32R = mybir.dt.float32r
BF16 = mybir.dt.bfloat16
I32 = mybir.dt.int32
EPS = 1e-5
LAYERS = 3
CONSTS = 12
DMA = 16
RANK_RING = 4
RANK_BANKS = 2
CHUNK = 4
CHUNKS = 2
EDGE_RING = 4
EDGE_BANKS = 2
NODE_RING = 4
NODE_STEPS_BESIDE = {-3: (-4,), -2: (-3,), -1: (-2, -1), 0: (0,)}
NODE_STEPS_AHEAD = 2
NODES_BESIDE = (NODE_RING, NODE_RING + 1)


def write_out(count, ring, body, part=lambda d: True):
    return lambda i: body(i // ring, i % ring, lambda d: 0 <= i + d < count and part(d))


def sweep(eng, count, ring, low, high, body, begin=None, beside=None):
    first, end = 1 - low // ring, (count - high) // ring
    step = write_out(count, ring, body)

    for i in range(-high if begin is None else begin, first * ring):
        step(i)
    with eng.Fori(first, end) as j:
        for s in range(ring):
            body(j, s, lambda d: True)
    for i in range(end * ring, count - low):
        step(i)
        if beside:
            beside(i)


def sage_kernel(nc, x_in, src_in, dst_in, weights, out):
    N, D = x_in.shape
    E = src_in.shape[0]
    K = D // P
    NODE_TILES = -(-N // P)
    LAST_ROWS = N - (NODE_TILES - 1) * P
    EDGE_TILES = -(-E // P)
    EDGES = EDGE_TILES * P
    EDGE_ROWS = E // EDGE_TILES
    PAD_NODE = NODE_TILES * P
    BIAS_ROW = EDGES
    HALF = EDGES // 2
    STEP = CHUNK * CHUNKS
    STEPS = EDGE_TILES // STEP
    assert EDGE_TILES % STEP == 0
    assert D == 512 and EDGE_ROWS * EDGE_TILES == E and EDGE_ROWS <= P and NODE_TILES < P and HALF < 4096

    with ExitStack() as ctx:
        def sb(name, shape, dt):
            return ctx.enter_context(nc.sbuf_tensor(name, shape, dt))

        def sem(name):
            return ctx.enter_context(nc.semaphore(name))

        def sems(name, n):
            return [sem(f"{name}{i}") for i in range(n)]

        node_x = nc.dram_tensor("node_x", [NODE_TILES * P, D], F32).ap()
        edge_table = nc.dram_tensor("edge_table", [EDGES + 1, D], F32).ap()

        bank = [ctx.enter_context(nc.psum_tensor(f"bank{i}", [P, 512], F32)) for i in range(8)]

        stage = {m: sb(f"stage_{m}", [P, K, D], F32) for m in "plr"}
        w_high = {m: sb(f"w_high_{m}", [P, K, D], F32R) for m in "plr"}
        w_low = {m: sb(f"w_low_{m}", [P, K, D], F32R) for m in "plr"}
        bias_stage = {m: sb(f"bias_stage_{m}", [P, D], F32) for m in "pl"}
        bias = {m: sb(f"bias_{m}", [P, D], F32) for m in "pl"}
        gain = sb("gain", [P, K], F32)
        shift = sb("shift", [P, K], F32)
        shift_cols = sb("shift_cols", [P, K, P], F32)

        ones = sb("ones", [P, P], F32)
        ident = sb("ident", [P, P], F32)
        below = sb("below", [P, P], F32)
        above = sb("above", [P, P], F32)
        upto = sb("upto", [P, P], F32)
        column_no = sb("column_no", [P, P], F32)
        partition_no = sb("partition_no", [P, 1], F32)
        eps = sb("eps", [P, 1], F32)
        ones_b = sb("ones_b", [P, P], BF16)
        digit_b = sb("digit_b", [P, P], BF16)
        ident_b = sb("ident_b", [P, P], BF16)

        dst_i = sb("dst_i", [P, EDGE_TILES], I32)
        src_i = sb("src_i", [P, EDGE_TILES], I32)
        hi_i = sb("hi_i", [P, EDGE_TILES], I32)
        lo_i = sb("lo_i", [P, EDGE_TILES], I32)
        dst_f = sb("dst_f", [P, EDGE_TILES], F32)
        hi_f = sb("hi_f", [P, EDGE_TILES], F32)
        lo_f = sb("lo_f", [P, EDGE_TILES], F32)
        edge_values = sb("edge_values", [P, EDGE_TILES, 3], F32)
        count_lh = sb("count_lh", [P, P], F32)
        count_hl = sb("count_hl", [P, P], F32)
        minus_half = sb("minus_half", [P, 1], F32)
        start = sb("start", [P, P], F32)
        column_total = sb("column_total", [P, 1], F32)
        tile_start = sb("tile_start", [P, 1], F32)
        total_cols = sb("total_cols", [P, P], F32)
        rank_start = sb("rank_start", [P, EDGE_TILES], F32)
        rank_in_tile = sb("rank_in_tile", [P, EDGE_TILES], F32)
        rank_i = sb("rank_i", [P, EDGE_TILES], I32)
        rank_hi = sb("rank_hi", [P, EDGE_TILES], F32)
        rank_lo = sb("rank_lo", [P, EDGE_TILES], F32)
        edge_count = sb("edge_count", [P, EDGE_TILES], F32)
        sorted_dst_i = sb("sorted_dst_i", [P, EDGE_TILES], I32)
        sorted_dst = sb("sorted_dst", [P, EDGE_TILES], F32)
        sorted_hi = sb("sorted_hi", [P, EDGE_TILES], F32)
        sorted_lo = sb("sorted_lo", [P, EDGE_TILES], F32)
        sorted_src = sb("sorted_src", [P, EDGE_TILES], I32)
        sorted_share = sb("sorted_share", [P, EDGE_TILES], F32)
        dst_row = sb("dst_row", [P, 1 + EDGES], F32)
        hot = dst_row[:, 1:1 + EDGES].bitcast(BF16).rearrange("p (a t c) -> p a t c", a=2, c=P)
        has_edges = sb("has_edges", [P, P], F32)
        owner_f = sb("owner_f", [P, P], F32)
        owner_f2 = sb("owner_f2", [P, P], F32)
        owner = sb("owner", [P, P], I32)

        gathered = sb("gathered", [P, EDGE_RING, D], F32)
        gather_idx = sb("gather_idx", [P, EDGE_RING], I32)
        same = sb("same", [P, EDGE_RING, P], F32R)
        carries = sb("carries", [P, EDGE_RING, P], F32)
        h_pre = sb("h_pre", [P, D], F32)
        h_high = sb("h_high", [P, D], F32R)
        h_low = sb("h_low", [P, D], F32R)
        agg = sb("agg", [P, EDGE_RING, K, P], F32)
        agg_high = sb("agg_high", [P, K, P], F32R)
        agg_low = sb("agg_low", [P, K, P], F32R)
        edge_out = sb("edge_out", [P, EDGE_RING, D], F32)

        xt_high = sb("xt_high", [P, NODE_RING, K, P], F32R)
        xt_low = sb("xt_low", [P, NODE_RING, K, P], F32R)

        x_tile = sb("x_tile", [P, NODE_RING, D], F32)
        residual = sb("residual", [P, NODE_RING, D], F32)
        owner_idx = sb("owner_idx", [P, NODE_RING], I32)
        edge_row = sb("edge_row", [P, NODE_RING, D], F32)
        y = sb("y", [P, NODE_RING, D], F32)

        def carve(buf, shapes):
            flat, at, views = buf[:].rearrange(buf_axes[len(buf[:].shape)]), 0, []
            for ring, width, dt in shapes:
                words = ring * width // (2 if dt == BF16 else 1)
                view = flat[:, at:at + words].bitcast(dt)
                views.append(view.rearrange("p (s c) -> p s c", s=ring))
                at += words
            assert at <= EDGE_RING * D
            return views

        buf_axes = {3: "p a b -> p (a b)", 4: "p a b c -> p (a b c)"}
        diag_hi, diag_lo, unused = carve(y, [
            (STEP, P, BF16),
            (STEP, P, BF16),
            (3 * RANK_RING, P, BF16)])
        hot_t, lookup = carve(xt_high, [
            (RANK_RING, P, F32R),
            (RANK_RING, 2 * P, F32R)])
        place, = carve(agg, [(STEP, P, F32)])
        place_tile, placed = carve(edge_out, [
            (STEP, EDGE_TILES, F32),
            (STEP, 3 * EDGE_TILES, F32)])

        in_stats = sb("in_stats", [P, NODE_RING, 6], F32)
        in_mean = sb("in_mean", [P, NODE_RING, 2], F32)
        in_std = sb("in_std", [P, NODE_RING], F32)
        in_rstd = sb("in_rstd", [P, NODE_RING], F32)
        in_off = sb("in_off", [P, NODE_RING], F32)
        ln_stats = sb("ln_stats", [P, NODE_RING, 6], F32)
        ln_mean = sb("ln_mean", [P, NODE_RING, 2], F32)
        ln_std = sb("ln_std", [P, NODE_RING], F32)
        ln_rstd = sb("ln_rstd", [P, NODE_RING], F32)
        ln_off = sb("ln_off", [P, NODE_RING], F32)

        w_loaded = {m: sem(f"w_loaded_{m}") for m in "plr"}
        bias_loaded = {m: sem(f"bias_loaded_{m}") for m in "pl"}
        affine_loaded = sem("affine_loaded")
        w_high_done = {m: sem(f"w_high_done_{m}") for m in "plr"}
        w_low_done = {m: sem(f"w_low_done_{m}") for m in "plr"}
        shift_done = sem("shift_done")
        bias_product = {m: sem(f"bias_product_{m}") for m in "pl"}
        bias_done = {m: sem(f"bias_done_{m}") for m in "pl"}
        bias_stored = sem("bias_stored")

        consts = sem("consts")
        memset_done = sem("memset_done")
        rows_cleared = sem("rows_cleared")
        pads_done = sem("pads_done")
        graph_loaded = sem("graph_loaded")
        digits = sem("digits")
        hot_done = sem("hot_done")
        counted = sem("counted")
        prep = sem("prep")
        prep_pe = sem("prep_pe")
        lookup_counts = sem("lookup_counts")
        diag_done = sem("diag_done")
        row_done = sem("row_done")
        hot_t_done = sem("hot_t_done")
        in_tile_done = sem("in_tile_done")
        table_copied = sem("table_copied")
        table_added = sem("table_added")
        looked_up = sem("looked_up")
        rank_read = sem("rank_read")
        rank_digits = sem("rank_digits")
        place_tile_done = sem("place_tile_done")
        placed_done = sem("placed_done")
        sorted_chunk = sem("sorted_chunk")
        sorted_copied = sem("sorted_copied")
        sorted_ready = sem("sorted_ready")
        sdiag_done = sem("sdiag_done")
        srow_done = sem("srow_done")
        srow_copied = sem("srow_copied")
        owner_ready = sem("owner_ready")

        e_idx = sem("e_idx")
        e_gathered = sems("e_gathered", EDGE_RING)
        e_turned = sem("e_turned")
        e_xt_high = sem("e_xt_high")
        e_xt_low = sem("e_xt_low")
        e_projected = sem("e_projected")
        e_h_pre = sem("e_h_pre")
        e_h_high = sem("e_h_high")
        e_h_low = sem("e_h_low")
        e_masks = sem("e_masks")
        e_summed = sem("e_summed")
        e_agg = sem("e_agg")
        e_agg_high = sem("e_agg_high")
        e_agg_low = sem("e_agg_low")
        e_product = sem("e_product")
        e_out = sem("e_out")
        e_stored = sems("e_stored", EDGE_RING)

        n_loaded = sems("n_loaded", NODE_RING)
        n_residual = sems("n_residual", NODE_RING)
        n_idx = sem("n_idx")
        n_gathered = sems("n_gathered", NODE_RING)
        n_turned = sem("n_turned")
        n_xt_high = sem("n_xt_high")
        n_xt_low = sem("n_xt_low")
        n_product = sem("n_product")
        n_summed = sem("n_summed")
        n_relu = sem("n_relu")
        n_stats = sem("n_stats")
        n_mean = sem("n_mean")
        n_std = sem("n_std")
        n_rstd = sem("n_rstd")
        n_off = sem("n_off")
        n_out = sem("n_out")
        n_stored = sems("n_stored", NODE_RING)

        in_s_stats = sem("in_s_stats")
        in_s_mean = sem("in_s_mean")
        in_s_std = sem("in_s_std")
        in_s_rstd = sem("in_s_rstd")
        in_s_off = sem("in_s_off")
        in_s_done = sem("in_s_done")

        def reach(eng, s, value):
            if not isinstance(value, int) or value > 0:
                eng.wait_ge(s, value)

        class Phase:

            def __init__(self, l, count, ring):
                self.l, self.count, self.ring = l, count, ring

            def at(self, j, s, d):
                return j * self.ring + (s + d), (s + d) % self.ring, j + (s + d) // self.ring

            def tiles(self, t):
                return t + (self.l * self.count + 1)

            def slot(self, slot, turn):
                per_layer = -(-(self.count - slot) // self.ring)
                return turn * DMA + (self.l * per_layer + 1) * DMA

        def ahead(d):
            return d > 0

        def behind(d):
            return d <= 0

        def over_tiles(row, count=CHUNK):
            return row.rearrange("p (t c) -> p t c", t=1).to_broadcast([P, count, row.shape[1]])

        def over_columns(values, columns=P):
            return values.rearrange("p (t c) -> p t c", c=1).to_broadcast([P, values.shape[1], columns])

        def edges(l):
            return Phase(l, EDGE_TILES, EDGE_RING)

        def nodes(l):
            return Phase(l, NODE_TILES, NODE_RING)

        def all_edge_rows_stored(eng, l):
            for s in range(EDGE_RING):
                eng.wait_ge(e_stored[s], DMA * (l + 1) * (-(-(EDGE_TILES - s) // EDGE_RING)))

        def all_nodes_stored(eng, l):
            for s in range(NODE_RING):
                eng.wait_ge(n_stored[s], DMA * (l + 1) * (-(-(NODE_TILES - s) // NODE_RING)))

        block = ctx.enter_context(nc.Block())

        @block.sync
        def _(sp):
            def load_weights(l, ms):
                for m in ms:
                    if l:
                        sp.wait_ge(w_low_done[m], K * l)
                        sp.wait_ge(w_high_done[m], K * l)
                        if l > 1 and m == "p":
                            sp.wait_ge(bias_product["p"], l - 1)
                        if l > 1 and m == "r":
                            sp.wait_ge(bias_product["l"], l - 1)
                    sp.dma_start(stage[m][:], weights[l]["W" + m].rearrange("(k p) n -> p k n", p=P)
                                 ).then_inc(w_loaded[m], DMA)

            def load_biases(l):
                for m in "pl":
                    if l:
                        sp.wait_ge(bias_done[m], l)
                    sp.dma_start(bias_stage[m][:], weights[l]["b" + m].rearrange("(a n) -> a n", a=1)
                                 .to_broadcast([P, D])).then_inc(bias_loaded[m], DMA)

            def load_affine(l):
                if l > 1:
                    sp.wait_ge(w_low_done["r"], K * l)
                    sp.wait_ge(w_high_done["r"], K * l)
                    sp.wait_ge(w_low_done["p"], K * l)
                    sp.wait_ge(shift_done, l - 1)
                for buf, name in ((gain, "g"), (shift, "be")):
                    sp.dma_start(buf[:], weights[l][name]).then_inc(affine_loaded, DMA)

            sp.wait_ge(pads_done, 2)
            sp.dma_start(dst_i[0:EDGE_ROWS, :], dst_in.rearrange("(p t) -> p t", t=EDGE_TILES)
                         ).then_inc(graph_loaded, DMA)
            sp.dma_start(src_i[0:EDGE_ROWS, :], src_in.rearrange("(p t) -> p t", t=EDGE_TILES)
                         ).then_inc(graph_loaded, DMA)
            load_weights(0, "plr")
            load_biases(0)
            for l in range(LAYERS):
                if l + 1 < LAYERS:
                    load_affine(l + 1)
                    load_weights(l + 1, "pl")
                sp.wait_ge(bias_done["l"], l + 1)
                sp.dma_start(edge_table[BIAS_ROW:BIAS_ROW + 1, :], bias["l"][0:1, :]
                             ).then_inc(bias_stored, DMA)
                source = x_in if l == 0 else node_x
                target = out if l == LAYERS - 1 else node_x

                def load_nodes(t, slot):
                    rows = P if not isinstance(t, int) or t < NODE_TILES - 1 or l else LAST_ROWS
                    sp.dma_start(x_tile[0:rows, slot, :], source[bass.ds(t * P, rows), :]
                                 ).then_inc(n_loaded[slot], DMA)

                if l:
                    all_nodes_stored(sp, l - 1)
                    sp.wait_ge(n_turned, NODE_TILES * l)
                else:
                    sp.wait_ge(rows_cleared, 2)
                for t in range(NODE_RING):
                    load_nodes(t, t)

                ph = edges(l)

                def store_edges(j, s, alive):
                    t, slot, turn = ph.at(j, s, 0)
                    sp.wait_ge(e_out, ph.tiles(t))
                    sp.dma_start(edge_table[bass.ds(t * P, P), :], edge_out[:, slot, :]
                                 ).then_inc(e_stored[slot], DMA)

                nph = nodes(l)

                def load_next(t):
                    sp.wait_ge(n_turned, nph.tiles(t - NODE_RING))
                    load_nodes(t, t % NODE_RING)

                def beside_edges(i):
                    if i == EDGE_TILES - 2:
                        for t in NODES_BESIDE:
                            load_next(t)

                sweep(sp, EDGE_TILES, EDGE_RING, 0, 2, store_edges, begin=0, beside=beside_edges)

                def move_nodes(j, s, alive):
                    if l + 1 < LAYERS and isinstance(j, int) and j * NODE_RING + s == NODE_RING:
                        load_biases(l + 1)
                        load_weights(l + 1, "r")
                    if alive(5) and (not isinstance(j, int) or j * NODE_RING + s + 5 > NODES_BESIDE[-1]):
                        t, slot, turn = nph.at(j, s, 5)
                        sp.wait_ge(n_turned, nph.tiles(t - NODE_RING))
                        load_nodes(t, slot)
                    if alive(-2):
                        t, slot, turn = nph.at(j, s, -2)
                        last = isinstance(t, int) and t == NODE_TILES - 1 and l == LAYERS - 1
                        rows = LAST_ROWS if last else P
                        sp.wait_ge(n_out, nph.tiles(t))
                        sp.dma_start(target[bass.ds(t * P, rows), :], y[0:rows, slot, :]
                                     ).then_inc(n_stored[slot], DMA)
                    if l == LAYERS - 1 and alive(3):
                        t, slot, turn = nph.at(j, s, 3)
                        rows = P if not isinstance(t, int) or t < NODE_TILES - 1 else LAST_ROWS
                        if not isinstance(t, int) or t >= NODE_RING:
                            sp.wait_ge(n_out, nph.tiles(t - NODE_RING))
                        sp.dma_start(residual[0:rows, slot, :], x_in[bass.ds(t * P, rows), :]
                                     ).then_inc(n_residual[slot], DMA)

                sweep(sp, NODE_TILES, NODE_RING, -2, 5, move_nodes)
            all_nodes_stored(sp, LAYERS - 1)

        @block.gpsimd
        def _(pool):
            def triangle(buf, compare, sign=1):
                nc.gpsimd.affine_select(out=buf[:], in_=ones[:], compare_op=compare, fill=0.0, base=0,
                                        pattern=[[sign, P]], channel_multiplier=-sign).then_inc(consts, 1)

            nc.gpsimd.memset(dst_i[:], PAD_NODE).then_inc(pads_done, 1)
            nc.gpsimd.memset(src_i[:], 0).then_inc(pads_done, 1)
            nc.gpsimd.memset(ones[:], 1.0).then_inc(memset_done, 1)
            pool.wait_ge(memset_done, 1)
            triangle(ident, ALU.is_equal)
            triangle(below, ALU.is_gt, -1)
            triangle(above, ALU.is_gt)
            triangle(upto, ALU.is_ge)
            nc.gpsimd.iota(column_no[:], pattern=[[1, P]], base=0, channel_multiplier=0,
                           allow_small_or_imprecise_dtypes=True).then_inc(consts, 1)
            nc.gpsimd.iota(partition_no[:], pattern=[[1, 1]], base=0, channel_multiplier=1,
                           allow_small_or_imprecise_dtypes=True).then_inc(consts, 1)
            nc.gpsimd.memset(eps[:], EPS).then_inc(consts, 1)
            nc.gpsimd.memset(ones_b[:], 1.0).then_inc(consts, 1)
            nc.gpsimd.memset(digit_b[:], float(P)).then_inc(consts, 1)
            nc.gpsimd.memset(minus_half[:], -float(HALF)).then_inc(consts, 1)
            nc.gpsimd.memset(ident_b[:], 0.0).then_inc(memset_done, 1)
            pool.wait_ge(memset_done, 2)
            nc.gpsimd.affine_select(out=ident_b[:], in_=ident_b[:], compare_op=ALU.not_equal, fill=1.0, base=0,
                                    pattern=[[1, P]], channel_multiplier=-1).then_inc(consts, 1)
            nc.gpsimd.memset(minus_half[:], -float(HALF)).then_inc(consts, 1)

            pool.wait_ge(digits, 6)
            pool.wait_ge(consts, CONSTS)

            def diagonals(j, c, first):
                chunk, slots = j * CHUNKS + c, slice(c * CHUNK, (c + 1) * CHUNK)
                tiles = bass.ds(chunk * CHUNK, CHUNK)
                if not first:
                    pool.wait_ge(row_done, (chunk - (CHUNKS - 1)) * CHUNK)
                for diag, digit in ((diag_hi, hi_f), (diag_lo, lo_f)):
                    last = nc.gpsimd.tensor_tensor(diag[:, slots, :], over_tiles(ident_b[:]),
                                                   over_columns(digit[:, tiles]), ALU.mult)
                last.then_inc(diag_done, 1)

            def low_halves(m):
                for k in range(K):
                    pool.wait_ge(w_high_done[m], k + 1)
                    nc.gpsimd.tensor_tensor(w_low[m][:, k, :], stage[m][:, k, :], w_high[m][:, k, :].bitcast(F32),
                                            ALU.subtract).then_inc(w_low_done[m], 1)

            for c in range(CHUNKS):
                diagonals(0, c, True)
            low_halves("p")
            low_halves("l")
            with pool.Fori(1, STEPS) as j:
                for c in range(CHUNKS):
                    diagonals(j, c, False)
            low_halves("r")
            nc.gpsimd.memset(x_tile[:], 0.0).then_inc(rows_cleared, 1)
            nc.gpsimd.memset(residual[:], 0.0).then_inc(rows_cleared, 1)

            def indexed(count, ring, ahead, copy, issue):
                def step(j, s, alive):
                    def tile(d):
                        return j + (s + d) // ring, (s + d) % ring, j * ring + (s + d)

                    if alive(ahead + 1) or alive(ahead):
                        copy(*tile(ahead + 1), alive(ahead + 1), alive(ahead))
                    if alive(ahead):
                        issue(*tile(ahead))

                sweep(pool, count, ring, ahead, ahead + 1, step)

            pool.wait_ge(sorted_ready, 1)
            for l in range(LAYERS):
                ph = edges(l)
                if l:
                    all_nodes_stored(pool, l - 1)

                def copy_index(ph, idx_copied, gathers, freed, idx_buf, table):
                    def copy(j, s, t, exists, before):
                        if before:
                            pool.wait_ge(idx_copied, ph.tiles(t - 1))
                            reach(pool, freed, ph.tiles(t - 1 - ph.ring))
                        if exists:
                            reach(pool, gathers[s], ph.slot(s, j - 1))
                            nc.gpsimd.tensor_copy(idx_buf[:, s:s + 1], table[:, bass.ds(t, 1)]
                                                  ).then_inc(idx_copied, 1)
                    return copy

                def gather_sources(j, s, t):
                    nc.gpsimd.indirect_dma_start(
                        out=gathered[:, s, :], out_offset=None, in_=x_in if l == 0 else node_x,
                        in_offset=bass.IndirectOffsetOnAxis(ap=gather_idx[:, s:s + 1], axis=0)
                    ).then_inc(e_gathered[s], DMA)

                indexed(EDGE_TILES, EDGE_RING, 4 if l == 0 else 3,
                        copy_index(ph, e_idx, e_gathered, e_turned, gather_idx, sorted_src), gather_sources)

                ph = nodes(l)
                if l == 0:
                    pool.wait_ge(owner_ready, 1)
                all_edge_rows_stored(pool, l)
                pool.wait_ge(bias_stored, DMA * (l + 1))

                def gather_edge_rows(j, s, t):
                    nc.gpsimd.indirect_dma_start(
                        out=edge_row[:, s, :], out_offset=None, in_=edge_table,
                        in_offset=bass.IndirectOffsetOnAxis(ap=owner_idx[:, s:s + 1], axis=0)
                    ).then_inc(n_gathered[s], DMA)

                indexed(NODE_TILES, NODE_RING, 0,
                        copy_index(ph, n_idx, n_gathered, n_summed, owner_idx, owner), gather_edge_rows)

        @block.tensor
        def _(pe):
            def split_product(psum, a_high, a_low, m):
                for k in range(K):
                    nc.tensor.matmul(psum, a_low[:, k, :], w_high[m][:, k, :], start=(k == 0), stop=False)
                    nc.tensor.matmul(psum, a_high[:, k, :], w_low[m][:, k, :], start=False, stop=False)
                    last = nc.tensor.matmul(psum, a_high[:, k, :], w_high[m][:, k, :],
                                            start=False, stop=(k == K - 1))
                return last

            def shift_product(m, of, l):
                pe.wait_ge(shift_done, l)
                pe.wait_ge(w_loaded[of], DMA * (l + 1))
                if l > 1:
                    pe.wait_ge(bias_done[m], l)
                for k in range(K):
                    last = nc.tensor.matmul(bank[6 if m == "p" else 7][:], shift_cols[:, k, :],
                                            stage[of][:, k, :], start=(k == 0), stop=(k == K - 1))
                last.then_inc(bias_product[m], 1)

            pe.wait_ge(consts, CONSTS)

            def count_chunk(chunk, first, last):
                pe.wait_ge(hot_done, chunk + 1)
                for i in range(CHUNK):
                    t = bass.ds(chunk * CHUNK + i, 1)
                    hot_hi, hot_lo = (hot[:, a, t, :].rearrange("p t c -> p (t c)") for a in range(2))
                    start, stop = first and i == 0, last and i == CHUNK - 1
                    nc.tensor.matmul(bank[0][:, 0:P], hot_lo, hot_hi, start=start, stop=stop, skip_group_check=True)
                    done = nc.tensor.matmul(bank[1][:, 0:P], hot_hi, hot_lo, start=start, stop=stop,
                                            skip_group_check=True)
                done.then_inc(counted, 1)

            for c in range(CHUNKS):
                count_chunk(c, c == 0, False)
            with pe.Fori(1, STEPS - 1) as j:
                for c in range(CHUNKS):
                    count_chunk(j * CHUNKS + c, False, False)
            for c in range(CHUNKS):
                count_chunk((STEPS - 1) * CHUNKS + c, False, c == CHUNKS - 1)

            pe.wait_ge(prep, 2)
            nc.tensor.matmul(bank[2][:, 0:P], above[:], count_hl[:], start=True, stop=True
                             ).then_inc(prep_pe, 1)
            nc.tensor.matmul(bank[3][:, 0:P], count_lh[:], above[:], start=True, stop=True
                             ).then_inc(prep_pe, 1)
            pe.wait_ge(prep, 6)
            nc.tensor.matmul(bank[4][:, 0:P], upto[:], count_lh[:], start=True, stop=False)
            nc.tensor.matmul(bank[4][:, 0:P], total_cols[:], above[:], start=False, stop=True
                             ).then_inc(prep_pe, 1)
            nc.tensor.matmul(bank[5][:, 0:P], ident[:], start[:], start=True, stop=False,
                             skip_group_check=True).then_inc(table_added, 1)

            def rank_step(j, s, alive):
                if alive(1):
                    t, slot = j * STEP + (s + 1), (s + 1) % STEP
                    if slot % CHUNK == 0:
                        pe.wait_ge(diag_done, j * CHUNKS + ((s + 1) // CHUNK + 1))
                    reach(pe, in_tile_done, t - 1)
                    reach(pe, hot_t_done, t - 1)
                    row = bank[slot % RANK_BANKS]
                    hot_hi = hot[:, 0, bass.ds(t, 1), :].rearrange("p t c -> p (t c)")
                    nc.tensor.matmul(row[:, 0:P], ones_b[:], diag_lo[:, slot, :], start=True, stop=False)
                    nc.tensor.matmul(row[:, 0:P], digit_b[:], diag_hi[:, slot, :], start=False, stop=True)
                    nc.tensor.matmul(bank[6 + slot % RANK_BANKS][:, 0:P], hot_hi, ident_b[:], start=True, stop=True
                                     ).then_inc(row_done, 1)
                if alive(0):
                    t, slot = j * STEP + s, s % RANK_RING
                    pe.wait_ge(table_copied, t + 1)
                    hot_hi, hot_lo = (hot[:, a, bass.ds(t, 1), :].rearrange("p t c -> p (t c)") for a in range(2))
                    nc.tensor.matmul(bank[5][:, 0:P], hot_hi, hot_lo, start=False,
                                     stop=False, skip_group_check=True).then_inc(table_added, 1)
                    pe.wait_ge(hot_t_done, t + 1)
                    reach(pe, rank_read, t - 1)
                    nc.tensor.matmul(bank[2 + slot % RANK_BANKS][:, 0:2 * P], hot_t[:, slot, :],
                                     lookup[:, slot, :], start=True, stop=True
                                     ).then_inc(looked_up, 1)

            sweep(pe, EDGE_TILES, STEP, 0, 1, rank_step)

            def sort_chunk(j, c, first, last):
                pe.wait_ge(placed_done, j * CHUNKS + (c + 1))
                for i in range(CHUNK):
                    slot = c * CHUNK + i
                    done = nc.tensor.matmul(bank[4][:, 0:3 * EDGE_TILES], place[:, slot, :], placed[:, slot, :],
                                            start=first and i == 0, stop=last and i == CHUNK - 1,
                                            skip_group_check=True)
                done.then_inc(sorted_chunk, 1)

            for c in range(CHUNKS):
                sort_chunk(0, c, c == 0, False)
            with pe.Fori(1, STEPS - 1) as j:
                for c in range(CHUNKS):
                    sort_chunk(j, c, False, False)
            for c in range(CHUNKS):
                sort_chunk(STEPS - 1, c, False, c == CHUNKS - 1)

            for l in range(LAYERS):
                ph = edges(l)
                if l:
                    pe.wait_ge(n_summed, NODE_TILES * l)
                    shift_product("p", "p", l)
                    shift_product("l", "r", l)
                for m in "pl":
                    pe.wait_ge(w_low_done[m], K * (l + 1))

                def sum_bank(slot):
                    return bank[4 if l == 0 else 4 + slot % EDGE_BANKS]

                def edge_step(j, s, alive):
                    if alive(1):
                        t, slot, turn = ph.at(j, s, 1)
                        if l == 0:
                            pe.wait_ge(in_s_done, t + 1)
                        else:
                            pe.wait_ge(e_gathered[slot], ph.slot(slot, turn))
                        reach(pe, e_xt_low, ph.tiles(t - EDGE_BANKS))
                        for k in range(K):
                            last = nc.tensor.transpose(bank[slot % EDGE_BANKS][:, k * P:(k + 1) * P],
                                                       gathered[:, slot, k * P:(k + 1) * P], ident[:])
                        last.then_inc(e_turned, 1)
                    if alive(-2):
                        t, slot, turn = ph.at(j, s, -2)
                        pe.wait_ge(e_agg_low, ph.tiles(t))
                        reach(pe, e_out, ph.tiles(t - EDGE_BANKS))
                        split_product(bank[6 + slot % EDGE_BANKS][:], agg_high, agg_low, "l").then_inc(e_product, 1)
                    if alive(-1):
                        t, slot, turn = ph.at(j, s, -1)
                        pe.wait_ge(e_masks, ph.tiles(t))
                        pe.wait_ge(e_h_low, ph.tiles(t))
                        reach(pe, e_agg, ph.tiles(t - (1 if l == 0 else EDGE_BANKS)))
                        for k in range(K):
                            cols = slice(k * P, (k + 1) * P)
                            nc.tensor.matmul(sum_bank(slot)[:, cols], h_low[:, cols], same[:, slot, :],
                                             start=True, stop=False)
                            last = nc.tensor.matmul(sum_bank(slot)[:, cols], h_high[:, cols],
                                                    same[:, slot, :], start=False, stop=True)
                        last.then_inc(e_summed, 1)
                    if l == 0 and alive(2):
                        t, slot, turn = ph.at(j, s, 2)
                        pe.wait_ge(sdiag_done, t + 1)
                        reach(pe, srow_copied, t)
                        cols = slice(slot * P, (slot + 1) * P)
                        nc.tensor.matmul(bank[5][:, cols], ones_b[:], diag_lo[:, slot, :], start=True, stop=False)
                        nc.tensor.matmul(bank[5][:, cols], digit_b[:], diag_hi[:, slot, :], start=False, stop=True
                                         ).then_inc(srow_done, 1)
                    if alive(0):
                        t, slot, turn = ph.at(j, s, 0)
                        pe.wait_ge(e_xt_low, ph.tiles(t))
                        reach(pe, e_h_pre, ph.tiles(t - EDGE_BANKS))
                        split_product(bank[2 + slot % EDGE_BANKS][:], xt_high[:, slot], xt_low[:, slot], "p"
                                      ).then_inc(e_projected, 1)

                nph = nodes(l)

                def node_step(j, s, alive):
                    if alive(2):
                        t, slot, turn = nph.at(j, s, 2)
                        if l == 0:
                            pe.wait_ge(in_s_done, t + (EDGE_TILES + 1))
                        else:
                            pe.wait_ge(n_loaded[slot], nph.slot(slot, turn))
                        reach(pe, n_xt_low, nph.tiles(t - NODE_RING))
                        for k in range(K):
                            last = nc.tensor.transpose(bank[slot][:, k * P:(k + 1) * P],
                                                       x_tile[:, slot, k * P:(k + 1) * P], ident[:])
                        last.then_inc(n_turned, 1)
                    if alive(0):
                        t, slot, turn = nph.at(j, s, 0)
                        if isinstance(t, int) and t == 0:
                            pe.wait_ge(w_low_done["r"], K * (l + 1))
                            pe.wait_ge(e_agg, EDGE_TILES * (l + 1))
                        pe.wait_ge(n_xt_low, nph.tiles(t))
                        reach(pe, n_summed, nph.tiles(t - NODE_RING))
                        split_product(bank[4 + slot][:], xt_high[:, slot], xt_low[:, slot], "r"
                                      ).then_inc(n_product, 1)

                def beside_edges(i):
                    for n in NODE_STEPS_BESIDE.get(i - EDGE_TILES, ()):
                        write_out(NODE_TILES, NODE_RING, node_step)(n)

                sweep(pe, EDGE_TILES, EDGE_RING, -2, 2 if l == 0 else 1, edge_step, beside=beside_edges)

                sweep(pe, NODE_TILES, NODE_RING, 0, 2, node_step, begin=1)

        @block.scalar
        def _(act):
            act.wait_ge(consts, CONSTS)

            def high_of(m, l, k):
                act.wait_ge(w_loaded[m], DMA * (l + 1))
                if l and m != "l":
                    act.wait_ge(affine_loaded, 2 * DMA * l)
                    scale = gain[:, k:k + 1]
                else:
                    scale = 1.0
                nc.scalar.activation(w_high[m][:, k, :], stage[m][:, k, :], ACT.Identity, scale=scale
                                     ).then_inc(w_high_done[m], 1)

            for m in "plr":
                for k in range(K):
                    high_of(m, 0, k)

            for m in "pl":
                act.wait_ge(bias_loaded[m], DMA)
                nc.scalar.activation(bias[m][:], bias_stage[m][:], ACT.Identity).then_inc(bias_done[m], 1)

            act.wait_ge(digits, 6)
            act.wait_ge(lookup_counts, RANK_RING)

            def rank_step(j, s, alive):
                if alive(0):
                    t, slot = j * STEP + s, s % RANK_RING
                    act.wait_ge(table_added, t + 1)
                    reach(act, looked_up, t - (RANK_RING - 1))
                    nc.scalar.activation(lookup[:, slot, 0:P], bank[5][:, 0:P], ACT.Identity, bias=minus_half[:]
                                         ).then_inc(table_copied, 1)
                if alive(1):
                    t, slot = j * STEP + (s + 1), (s + 1) % RANK_RING
                    act.wait_ge(row_done, t + 1)
                    reach(act, looked_up, t - (RANK_RING - 1))
                    nc.scalar.activation(hot_t[:, slot, :], bank[6 + slot % RANK_BANKS][:, 0:P], ACT.Identity
                                         ).then_inc(hot_t_done, 1)

            sweep(act, EDGE_TILES, STEP, 0, 1, rank_step)
            act.wait_ge(sorted_copied, 7)

            def in_std_of(t, base, slot):
                act.wait_ge(in_s_mean, t + (base + 1))
                nc.scalar.activation(in_std[:, slot:slot + 1], in_mean[:, slot, 1:2], ACT.Sqrt,
                                     bias=eps[:]).then_inc(in_s_std, 1)

            def in_centre(t, base, slot, buf):
                act.wait_ge(in_s_off, t + (base + 1))
                nc.scalar.activation(buf[:, slot, :], buf[:, slot, :], ACT.Identity,
                                     bias=in_off[:, slot:slot + 1]).then_inc(in_s_done, 1)

            for l in range(LAYERS):
                ph = edges(l)
                turned_act = ACT.Relu if l == 0 else ACT.Identity
                if l:
                    act.wait_ge(n_product, NODE_TILES * l)

                def edge_step(j, s, alive):
                    if l == 0 and alive(2):
                        t, slot, turn = ph.at(j, s, 2)
                        in_std_of(t, 0, slot)
                    if alive(1):
                        t, slot, turn = ph.at(j, s, 1)
                        act.wait_ge(e_turned, ph.tiles(t))
                        reach(act, e_projected, ph.tiles(t - EDGE_RING))
                        nc.scalar.activation(xt_high[:, slot].rearrange("p k m -> p (k m)"),
                                             bank[slot % EDGE_BANKS][:], turned_act).then_inc(e_xt_high, 1)
                    if l == 0 and alive(2):
                        t, slot, turn = ph.at(j, s, 2)
                        in_centre(t, 0, slot, gathered)
                    if alive(-1):
                        t, slot, turn = ph.at(j, s, -1)
                        act.wait_ge(e_agg, ph.tiles(t))
                        reach(act, e_product, ph.tiles(t - 1))
                        nc.scalar.activation(agg_high[:], agg[:, slot], ACT.Identity).then_inc(e_agg_high, 1)
                    if alive(0):
                        t, slot, turn = ph.at(j, s, 0)
                        act.wait_ge(e_h_pre, ph.tiles(t))
                        reach(act, e_summed, ph.tiles(t - 1))
                        nc.scalar.activation(h_high[:], h_pre[:], ACT.Relu).then_inc(e_h_high, 1)
                    if l == 0 and alive(2):
                        t, slot, turn = ph.at(j, s, 2)
                        act.wait_ge(srow_done, t + 1)
                        nc.scalar.activation(dst_row[:, bass.ds(t * P + 1, P)], bank[5][:, slot * P:(slot + 1) * P],
                                             ACT.Identity).then_inc(srow_copied, 1)
                    if l == 0 and alive(3):
                        t, slot, turn = ph.at(j, s, 3)
                        reach(act, srow_done, t - (EDGE_RING - 1))
                        nc.scalar.activation(diag_hi[:, slot, :], ident_b[:], ACT.Identity,
                                             scale=sorted_hi[:, bass.ds(t, 1)])
                        nc.scalar.activation(diag_lo[:, slot, :], ident_b[:], ACT.Identity,
                                             scale=sorted_lo[:, bass.ds(t, 1)]).then_inc(sdiag_done, 1)
                    if l and isinstance(j, int) and 0 <= j * EDGE_RING + s < K:
                        high_of("r", l, j * EDGE_RING + s)

                nph = nodes(l)

                def node_step(j, s, alive):
                    if alive(2):
                        t, slot, turn = nph.at(j, s, 2)
                        if isinstance(t, int) and t == 0:
                            act.wait_ge(e_projected, EDGE_TILES * (l + 1))
                        act.wait_ge(n_turned, nph.tiles(t))
                        reach(act, n_product, nph.tiles(t - NODE_RING))
                        nc.scalar.activation(xt_high[:, slot].rearrange("p k m -> p (k m)"), bank[slot][:],
                                             turned_act).then_inc(n_xt_high, 1)
                    if l == 0 and alive(3):
                        t, slot, turn = nph.at(j, s, 3)
                        in_std_of(t, EDGE_TILES, slot)
                    if l + 1 < LAYERS and alive(-2):
                        t, slot, turn = nph.at(j, s, -2)
                        act.wait_ge(n_mean, nph.tiles(t))
                        nc.scalar.activation(ln_std[:, slot:slot + 1], ln_mean[:, slot, 1:2], ACT.Sqrt,
                                             bias=eps[:]).then_inc(n_std, 1)
                    if l + 1 < LAYERS and alive(-1):
                        t, slot, turn = nph.at(j, s, -1)
                        act.wait_ge(n_summed, nph.tiles(t))
                        nc.scalar.activation(y[:, slot, :], y[:, slot, :], ACT.Relu).then_inc(n_relu, 1)
                    if l == 0 and alive(3):
                        t, slot, turn = nph.at(j, s, 3)
                        in_centre(t, EDGE_TILES, slot, x_tile)
                    if l == 0 and alive(-2):
                        t, slot, turn = nph.at(j, s, -2)
                        act.wait_ge(n_off, nph.tiles(t))
                        nc.scalar.activation(y[:, slot, :], y[:, slot, :], ACT.Identity,
                                             bias=ln_off[:, slot:slot + 1], scale=ln_rstd[:, slot:slot + 1]
                                             ).then_inc(n_out, 1)
                    if l + 1 < LAYERS and alive(0) and isinstance(j, int) and j * NODE_RING + s < 2 * K:
                        i = j * NODE_RING + s
                        high_of("pl"[i // K], l + 1, i % K)

                def beside_edges(i):
                    for n in NODE_STEPS_BESIDE.get(i - EDGE_TILES, ()):
                        write_out(NODE_TILES, NODE_RING, node_step, ahead)(n)

                sweep(act, EDGE_TILES, EDGE_RING, -1, 3 if l == 0 else 1, edge_step, beside=beside_edges)

                act.wait_ge(e_product, EDGE_TILES * (l + 1))

                for n in range(1, NODE_STEPS_AHEAD):
                    write_out(NODE_TILES, NODE_RING, node_step, ahead)(n)
                for n in range(NODE_STEPS_AHEAD):
                    write_out(NODE_TILES, NODE_RING, node_step, behind)(n)
                sweep(act, NODE_TILES, NODE_RING, -2 if l + 1 < LAYERS else 0, 3 if l == 0 else 2, node_step,
                      begin=NODE_STEPS_AHEAD)

        @block.vector
        def _(dve):
            V = nc.vector
            dve.wait_ge(consts, CONSTS)
            V.memset(dst_row[:, 0:1], -1.0).then_inc(digits, 1)

            def low_of(m, l, k):
                dve.wait_ge(w_high_done[m], K * l + k + 1)
                scaled = l and m != "l"
                V.scalar_tensor_tensor(out=w_low[m][:, k, :], in0=stage[m][:, k, :],
                                       scalar=gain[:, k:k + 1] if scaled else 1.0,
                                       in1=w_high[m][:, k, :].bitcast(F32), op0=ALU.mult, op1=ALU.subtract
                                       ).then_inc(w_low_done[m], 1)

            def shifted_bias(m, l):
                dve.wait_ge(bias_loaded[m], DMA * (l + 1))
                dve.wait_ge(bias_product[m], l)
                V.tensor_tensor(bias[m][:], bank[6 if m == "p" else 7][:], bias_stage[m][:], ALU.add
                                ).then_inc(bias_done[m], 1)

            dve.wait_ge(graph_loaded, 2 * DMA)
            V.tensor_scalar(hi_i[:], dst_i[:], 7, None, ALU.arith_shift_right).then_inc(digits, 1)
            V.tensor_scalar(lo_i[:], dst_i[:], 127, None, ALU.bitwise_and).then_inc(digits, 1)
            V.tensor_copy(dst_f[:], dst_i[:]).then_inc(digits, 1)
            dve.wait_ge(digits, 4)
            V.tensor_copy(hi_f[:], hi_i[:]).then_inc(digits, 1)
            V.tensor_copy(lo_f[:], lo_i[:]).then_inc(digits, 1)
            dve.wait_ge(digits, 6)

            with dve.Fori(0, STEPS) as j:
                for c in range(CHUNKS):
                    t = bass.ds(j * STEP + c * CHUNK, CHUNK)
                    for a, digit in enumerate((hi_f, lo_f)):
                        last = V.tensor_tensor(hot[:, a, t, :], over_tiles(column_no[:]), over_columns(digit[:, t]),
                                               ALU.is_equal)
                    last.then_inc(hot_done, 1)

            dve.wait_ge(counted, STEPS * CHUNKS)
            V.tensor_copy(count_lh[:], bank[0][:, 0:P]).then_inc(prep, 1)
            V.tensor_copy(count_hl[:], bank[1][:, 0:P]).then_inc(prep, 1)
            dve.wait_ge(prep_pe, 2)
            dve.wait_ge(prep, 2)
            V.tensor_reduce(tile_start[:], bank[2][:, 0:P], mybir.AxisListType.X, ALU.add).then_inc(prep, 1)
            V.tensor_reduce(column_total[:], count_hl[:], mybir.AxisListType.X, ALU.add).then_inc(prep, 1)
            dve.wait_ge(prep, 4)
            V.tensor_scalar(start[:], bank[3][:, 0:P], tile_start[:], None, ALU.add).then_inc(prep, 1)
            V.tensor_scalar(total_cols[:], ones[:], column_total[:], None, ALU.mult).then_inc(prep, 1)
            for s in range(RANK_RING):
                V.tensor_scalar(lookup[:, s, P:2 * P], count_hl[:], -float(HALF), None, ALU.add
                                ).then_inc(lookup_counts, 1)
            dve.wait_ge(prep_pe, 3)
            V.tensor_scalar(has_edges[:], count_lh[:], 0.0, None, ALU.is_gt).then_inc(prep, 1)
            V.tensor_scalar(owner_f[:], bank[4][:, 0:P], -1.0 - BIAS_ROW, None, ALU.add).then_inc(prep, 1)
            dve.wait_ge(prep, 8)
            V.tensor_tensor(owner_f2[:], owner_f[:], has_edges[:], ALU.mult).then_inc(prep, 1)
            dve.wait_ge(prep, 9)
            V.tensor_scalar(owner[:], owner_f2[:], float(BIAS_ROW), None, ALU.add).then_inc(owner_ready, 1)

            V.tensor_copy(edge_values[:, :, 0], src_i[:]).then_inc(prep, 1)
            V.tensor_copy(edge_values[:, :, 1], dst_f[:]).then_inc(prep, 1)

            def rank_step(j, s, alive):
                if alive(1):
                    t, slot = j * STEP + (s + 1), (s + 1) % RANK_RING
                    dve.wait_ge(row_done, t + 1)
                    V.scalar_tensor_tensor(out=unused[:, slot, :], in0=bank[slot % RANK_BANKS][:, 0:P],
                                           scalar=dst_f[:, bass.ds(t, 1)], in1=below[:], op0=ALU.is_equal,
                                           op1=ALU.mult, accum_out=rank_in_tile[:, bass.ds(t, 1)]
                                           ).then_inc(in_tile_done, 1)
                if alive(0):
                    t, slot = j * STEP + s, s % RANK_RING
                    col = bass.ds(t, 1)
                    dve.wait_ge(looked_up, t + 1)
                    for i, found in enumerate((rank_start, edge_count)):
                        last = V.scalar_tensor_tensor(
                            out=unused[:, (1 + i) * RANK_RING + slot, :],
                            in0=bank[2 + slot % RANK_BANKS][:, i * P:(i + 1) * P], scalar=1.0,
                            in1=hot[:, 1, col, :].rearrange("p t c -> p (t c)"), op0=ALU.mult, op1=ALU.mult,
                            accum_out=found[:, col])
                    last.then_inc(rank_read, 1)

            sweep(dve, EDGE_TILES, STEP, 0, 1, rank_step)
            dve.wait_ge(rank_read, EDGE_TILES)
            dve.wait_ge(prep, 11)

            V.scalar_tensor_tensor(out=rank_i[:], in0=rank_start[:], scalar=float(HALF), in1=rank_in_tile[:],
                                   op0=ALU.add, op1=ALU.add).then_inc(rank_digits, 1)
            V.tensor_scalar(edge_values[:, :, 2], edge_count[:], float(HALF), None, ALU.add).then_inc(rank_digits, 1)
            dve.wait_ge(rank_digits, 2)
            V.tensor_scalar(hi_i[:], rank_i[:], 7, None, ALU.arith_shift_right).then_inc(rank_digits, 1)
            V.tensor_scalar(lo_i[:], rank_i[:], 127, None, ALU.bitwise_and).then_inc(rank_digits, 1)
            dve.wait_ge(rank_digits, 4)
            V.tensor_copy(rank_hi[:], hi_i[:]).then_inc(rank_digits, 1)
            V.tensor_copy(rank_lo[:], lo_i[:]).then_inc(rank_digits, 1)
            dve.wait_ge(rank_digits, 6)

            def bring(j, c, first):
                chunk, slots = j * CHUNKS + c, slice(c * CHUNK, (c + 1) * CHUNK)
                t = bass.ds(j * STEP + c * CHUNK, CHUNK)
                if not first:
                    dve.wait_ge(sorted_chunk, chunk - (CHUNKS - 1))
                V.tensor_tensor(place_tile[:, slots, :], over_tiles(column_no[:, 0:EDGE_TILES]),
                                over_columns(rank_hi[:, t], EDGE_TILES), ALU.is_equal).then_inc(place_tile_done, 1)
                V.tensor_tensor(place[:, slots, :], over_tiles(column_no[:]), over_columns(rank_lo[:, t]),
                                ALU.is_equal)
                dve.wait_ge(place_tile_done, chunk + 1)
                V.tensor_tensor(
                    placed[:, slots, :].rearrange("p t (v c) -> p t v c", v=3),
                    place_tile[:, slots, :].rearrange("p t (v c) -> p t v c", v=1)
                    .to_broadcast([P, CHUNK, 3, EDGE_TILES]),
                    edge_values[:, t, :].rearrange("p t (v c) -> p t v c", c=1)
                    .to_broadcast([P, CHUNK, 3, EDGE_TILES]), ALU.mult).then_inc(placed_done, 1)

            for c in range(CHUNKS):
                bring(0, c, True)
            with dve.Fori(1, STEPS) as j:
                for c in range(CHUNKS):
                    bring(j, c, False)

            dve.wait_ge(sorted_chunk, STEPS * CHUNKS)
            field = [bank[4][:, i * EDGE_TILES:(i + 1) * EDGE_TILES] for i in range(3)]
            V.tensor_copy(sorted_src[:], field[0]).then_inc(sorted_ready, 1)
            V.tensor_copy(sorted_dst_i[:], field[1]).then_inc(sorted_copied, 1)
            V.tensor_copy(sorted_dst[:], field[1]).then_inc(sorted_copied, 1)
            V.reciprocal(sorted_share[:], field[2]).then_inc(sorted_copied, 1)
            dve.wait_ge(sorted_copied, 3)
            V.tensor_scalar(hi_i[:], sorted_dst_i[:], 7, None, ALU.arith_shift_right).then_inc(sorted_copied, 1)
            V.tensor_scalar(lo_i[:], sorted_dst_i[:], 127, None, ALU.bitwise_and).then_inc(sorted_copied, 1)
            dve.wait_ge(sorted_copied, 5)
            V.tensor_copy(sorted_hi[:], hi_i[:]).then_inc(sorted_copied, 1)
            V.tensor_copy(sorted_lo[:], lo_i[:]).then_inc(sorted_copied, 1)
            dve.wait_ge(sorted_copied, 7)

            def stats(buf, out_stats, slot, done):
                V.bn_stats(out_stats[:, slot, :], buf[:, slot, :]).then_inc(done, 1)

            def moments(out_mean, in_s, slot, done):
                V.bn_aggr(out_mean[:, slot, :], in_s[:, slot, :]).then_inc(done, 1)

            def in_scale(t, base, slot):
                dve.wait_ge(in_s_std, t + (base + 1))
                V.reciprocal(in_rstd[:, slot:slot + 1], in_std[:, slot:slot + 1]).then_inc(in_s_rstd, 1)

            def in_offset(t, base, slot):
                dve.wait_ge(in_s_mean, t + (base + 1))
                V.tensor_scalar(in_off[:, slot:slot + 1], in_mean[:, slot, 0:1], -1.0, None, ALU.mult
                                ).then_inc(in_s_off, 1)

            def xt_low_of(l, slot, bank_no):
                turned = bank[bank_no][:]
                high = xt_high[:, slot].rearrange("p k m -> p (k m)").bitcast(F32)
                low = xt_low[:, slot].rearrange("p k m -> p (k m)")
                if l == 0:
                    return V.scalar_tensor_tensor(out=low, in0=turned, scalar=0.0, in1=high,
                                                  op0=ALU.max, op1=ALU.subtract)
                return V.tensor_tensor(low, turned, high, ALU.subtract)

            for l in range(LAYERS):
                if l:
                    shifted_bias("l", l)
                    shifted_bias("p", l)
                ph = edges(l)

                def sum_bank(slot):
                    return bank[4 if l == 0 else 4 + slot % EDGE_BANKS]

                def edge_step(j, s, alive):
                    if l == 0 and alive(1):
                        t, slot, turn = ph.at(j, s, 1)
                        in_scale(t, 0, slot)
                    if alive(0):
                        t, slot, turn = ph.at(j, s, 0)
                        reach(dve, e_summed, ph.tiles(t - EDGE_RING))
                        if l == 0:
                            dve.wait_ge(srow_copied, t + 1)
                        row = dst_row[:, bass.ds(t * P + 1, P)]
                        V.tensor_scalar(same[:, slot, :], row, sorted_dst[:, bass.ds(t, 1)], None, ALU.is_equal)
                        V.tensor_scalar(carries[:, slot, :], row, dst_row[:, bass.ds(t * P, 1)], None,
                                        ALU.is_equal).then_inc(e_masks, 1)
                    if l == 0 and alive(2):
                        t, slot, turn = ph.at(j, s, 2)
                        in_offset(t, 0, slot)
                    if l == 0 and alive(3):
                        t, slot, turn = ph.at(j, s, 3)
                        dve.wait_ge(e_gathered[slot], ph.slot(slot, turn))
                        stats(gathered, in_stats, slot, in_s_stats)
                    if alive(1):
                        t, slot, turn = ph.at(j, s, 1)
                        if l == 0 and alive(3):
                            dve.wait_ge(in_s_stats, t + 3)
                        dve.wait_ge(e_xt_high, ph.tiles(t))
                        xt_low_of(l, slot, slot % EDGE_BANKS).then_inc(e_xt_low, 1)
                    elif l == 0 and alive(3):
                        dve.drain()
                    if l == 0 and alive(3):
                        t, slot, turn = ph.at(j, s, 3)
                        moments(in_mean, in_stats, slot, in_s_mean)
                    if alive(-1):
                        t, slot, turn = ph.at(j, s, -1)
                        dve.wait_ge(e_summed, ph.tiles(t))
                        if isinstance(t, int) and t == 0:
                            V.tensor_copy(agg[:, slot].rearrange("p k m -> p (k m)"), sum_bank(slot)[:]
                                          ).then_inc(e_agg, 1)
                        else:
                            dve.wait_ge(e_agg, ph.tiles(t - 1))
                            dve.wait_ge(e_masks, ph.tiles(t))
                            for k in range(K):
                                last = V.scalar_tensor_tensor(
                                    out=agg[:, slot, k, :], in0=carries[:, slot, :],
                                    scalar=agg[:, (slot - 1) % EDGE_RING, k, P - 1:P],
                                    in1=sum_bank(slot)[:, k * P:(k + 1) * P], op0=ALU.mult, op1=ALU.add)
                            last.then_inc(e_agg, 1)
                    if alive(-2):
                        t, slot, turn = ph.at(j, s, -2)
                        dve.wait_ge(e_product, ph.tiles(t))
                        reach(dve, e_stored[slot], ph.slot(slot, turn - 1))
                        V.scalar_tensor_tensor(out=edge_out[:, slot, :], in0=bank[6 + slot % EDGE_BANKS][:],
                                               scalar=sorted_share[:, bass.ds(t, 1)], in1=bias["l"][:],
                                               op0=ALU.mult, op1=ALU.add).then_inc(e_out, 1)
                    if alive(-1):
                        t, slot, turn = ph.at(j, s, -1)
                        dve.wait_ge(e_agg_high, ph.tiles(t))
                        V.tensor_tensor(agg_low[:], agg[:, slot], agg_high[:].bitcast(F32), ALU.subtract
                                        ).then_inc(e_agg_low, 1)
                    if alive(0):
                        t, slot, turn = ph.at(j, s, 0)
                        dve.wait_ge(e_projected, ph.tiles(t))
                        reach(dve, e_h_low, ph.tiles(t - 1))
                        if l == 0:
                            dve.wait_ge(in_s_rstd, t + 1)
                            last = V.scalar_tensor_tensor(
                                out=h_pre[:], in0=bank[2 + slot % EDGE_BANKS][:], scalar=in_rstd[:, slot:slot + 1],
                                in1=bias["p"][:], op0=ALU.mult, op1=ALU.add)
                        else:
                            last = V.tensor_tensor(h_pre[:], bank[2 + slot % EDGE_BANKS][:], bias["p"][:], ALU.add)
                        last.then_inc(e_h_pre, 1)
                        dve.wait_ge(e_h_high, ph.tiles(t))
                        V.scalar_tensor_tensor(out=h_low[:], in0=h_pre[:], scalar=0.0,
                                               in1=h_high[:].bitcast(F32), op0=ALU.max, op1=ALU.subtract
                                               ).then_inc(e_h_low, 1)
                    if l and isinstance(j, int) and 0 <= j * EDGE_RING + s < K:
                        low_of("r", l, j * EDGE_RING + s)

                nph = nodes(l)

                def node_step(j, s, alive):
                    norms = l + 1 < LAYERS
                    if l == 0 and alive(4):
                        t, slot, turn = nph.at(j, s, 4)
                        dve.wait_ge(n_loaded[slot], nph.slot(slot, turn))
                        stats(x_tile, in_stats, slot, in_s_stats)
                    if l == 0 and alive(-2):
                        t, slot, turn = nph.at(j, s, -2)
                        dve.wait_ge(n_std, nph.tiles(t))
                        V.reciprocal(ln_rstd[:, slot:slot + 1], ln_std[:, slot:slot + 1]).then_inc(n_rstd, 1)
                    if l == 0 and alive(3):
                        t, slot, turn = nph.at(j, s, 3)
                        in_offset(t, EDGE_TILES, slot)
                    if l == 0 and alive(-2):
                        t, slot, turn = nph.at(j, s, -2)
                        dve.wait_ge(n_rstd, nph.tiles(t))
                        V.scalar_tensor_tensor(out=ln_off[:, slot:slot + 1], in0=ln_mean[:, slot, 0:1],
                                               scalar=-1.0, in1=ln_rstd[:, slot:slot + 1], op0=ALU.mult,
                                               op1=ALU.mult).then_inc(n_off, 1)
                    if alive(2):
                        t, slot, turn = nph.at(j, s, 2)
                        if l == 0 and alive(4):
                            dve.wait_ge(in_s_stats, t + (EDGE_TILES + 3))
                        dve.wait_ge(n_xt_high, nph.tiles(t))
                        xt_low_of(l, slot, slot).then_inc(n_xt_low, 1)
                    elif l == 0 and alive(4):
                        dve.drain()
                    if 0 < l < LAYERS - 1 and alive(-2):
                        t, slot, turn = nph.at(j, s, -2)
                        dve.wait_ge(n_std, nph.tiles(t))
                        V.reciprocal(ln_rstd[:, slot:slot + 1], ln_std[:, slot:slot + 1]).then_inc(n_rstd, 1)
                    if norms and alive(-1):
                        t, slot, turn = nph.at(j, s, -1)
                        dve.wait_ge(n_relu, nph.tiles(t))
                        stats(y, ln_stats, slot, n_stats)
                    if l == 0 and alive(4):
                        t, slot, turn = nph.at(j, s, 4)
                        moments(in_mean, in_stats, slot, in_s_mean)
                    if l == 0 and alive(2):
                        t, slot, turn = nph.at(j, s, 2)
                        in_scale(t, EDGE_TILES, slot)
                    if 0 < l < LAYERS - 1 and alive(-2):
                        t, slot, turn = nph.at(j, s, -2)
                        dve.wait_ge(n_rstd, nph.tiles(t))
                        V.tensor_scalar(y[:, slot, :], y[:, slot, :], ln_mean[:, slot, 0:1],
                                        ln_rstd[:, slot:slot + 1], ALU.subtract, ALU.mult
                                        ).then_inc(n_out, 1)
                    if alive(0):
                        t, slot, turn = nph.at(j, s, 0)
                        if norms and alive(-1):
                            dve.wait_ge(n_stats, nph.tiles(t - 1))
                        dve.wait_ge(n_product, nph.tiles(t))
                        dve.wait_ge(n_gathered[slot], nph.slot(slot, turn))
                        reach(dve, n_stored[slot], nph.slot(slot, turn - 1))
                        if l == 0:
                            dve.wait_ge(in_s_rstd, t + (EDGE_TILES + 1))
                            last = V.scalar_tensor_tensor(
                                out=y[:, slot, :], in0=bank[4 + slot][:], scalar=in_rstd[:, slot:slot + 1],
                                in1=edge_row[:, slot, :], op0=ALU.mult, op1=ALU.add)
                        else:
                            last = V.tensor_tensor(y[:, slot, :], bank[4 + slot][:], edge_row[:, slot, :], ALU.add)
                        last.then_inc(n_summed, 1)
                        if l == LAYERS - 1:
                            dve.wait_ge(n_summed, nph.tiles(t))
                            last_layer = Phase(0, NODE_TILES, NODE_RING)
                            dve.wait_ge(n_residual[slot], last_layer.slot(slot, turn))
                            V.tensor_tensor(y[:, slot, :], y[:, slot, :], residual[:, slot, :], ALU.add
                                            ).then_inc(n_out, 1)
                    elif norms and alive(-1):
                        dve.drain()
                    if norms and alive(-1):
                        t, slot, turn = nph.at(j, s, -1)
                        moments(ln_mean, ln_stats, slot, n_mean)
                    if l + 1 < LAYERS and alive(0) and isinstance(j, int) and j * NODE_RING + s < 2 * K:
                        i = j * NODE_RING + s
                        low_of("pl"[i // K], l + 1, i % K)

                def beside_edges(i):
                    for n in NODE_STEPS_BESIDE.get(i - EDGE_TILES, ()):
                        write_out(NODE_TILES, NODE_RING, node_step, ahead)(n)

                sweep(dve, EDGE_TILES, EDGE_RING, -2, 3 if l == 0 else 1, edge_step, beside=beside_edges)

                if l + 1 < LAYERS:
                    dve.wait_ge(affine_loaded, 2 * DMA * (l + 1))
                    for k in range(K):
                        last = V.tensor_scalar(shift_cols[:, k, :], ones[:], shift[:, k:k + 1], None, ALU.mult)
                    last.then_inc(shift_done, 1)

                for n in range(1, NODE_STEPS_AHEAD):
                    write_out(NODE_TILES, NODE_RING, node_step, ahead)(n)
                for n in range(NODE_STEPS_AHEAD):
                    write_out(NODE_TILES, NODE_RING, node_step, behind)(n)
                sweep(dve, NODE_TILES, NODE_RING, -2 if l + 1 < LAYERS else 0, 4 if l == 0 else 2, node_step,
                      begin=NODE_STEPS_AHEAD)


def kernel(**inputs):
    import numpy as np
    import concourse.bacc as bacc
    from concourse.bass_utils import run_bass_kernel_spmd

    nc = bacc.Bacc("TRN2", target_bir_lowering=False, num_devices=1)
    arrays = {}

    def given(name, a):
        a = np.ascontiguousarray(a)
        arrays[name] = a
        return nc.dram_tensor(name, a.shape, mybir.dt.from_np(a.dtype), kind="ExternalInput").ap()

    x = given("x", inputs["x"])
    src = given("src", inputs["src"])
    dst = given("dst", inputs["dst"])
    weights = []
    for l in range(LAYERS):
        w = {}
        for m in "plr":
            w["W" + m] = given(f"W{m}{l}_t", np.asarray(inputs[f"L0_gnn_W{m}{l}"]).T)
        for m in "pl":
            w["b" + m] = given(f"b{m}{l}", inputs[f"L0_gnn_b{m}{l}"])
        if l:
            for name in ("g", "be"):
                column = np.asarray(inputs[f"L0_gnn_{name}{l - 1}"]).reshape(-1, P).T
                w[name] = given(f"{name}{l - 1}", column)
        weights.append(w)
    out = nc.dram_tensor("out", arrays["x"].shape, F32, kind="ExternalOutput").ap()
    sage_kernel(nc, x, src, dst, weights, out)
    r = run_bass_kernel_spmd(nc, [arrays], core_ids=[0])
    return r.results[0]["out"]
```
